# Optimizing a Trainium2 kernel written in Bass

```python
import numpy as np
import jax
import jax.numpy as jnp

def _softmax(x, axis=-1):
    return jax.nn.softmax(x, axis=axis)

def _gelu(x):
    return jax.nn.gelu(x, approximate=True)

def _silu(x):
    return jax.nn.silu(x)

def _sigmoid(x):
    return jax.nn.sigmoid(x)

def _layernorm(x, axis=-1, eps=1e-05):
    m = jnp.mean(x, axis=axis, keepdims=True)
    v = jnp.var(x, axis=axis, keepdims=True)
    return (x - m) / jnp.sqrt(v + eps)

def _scatter_add(tgt, idx, src, axis=0):
    return tgt.at[idx].add(src)

def _segment_sum(src, seg, n):
    return jax.ops.segment_sum(src, seg, n)
kernel_name = 'mk_early_fusion_d1_tok_img768_r4_1a9aac'

def setup_inputs(seed: int=0):
    np.random.seed(seed)
    _w = jnp.asarray

    def _rec_inputs():
        import jax
        import jax.numpy as jnp
        _rk = jax.random.key(seed)
        x = -0.000596345 + 1.00056 * jax.random.normal(jax.random.fold_in(_rk, 1), (2, 3, 64, 64), jnp.float32)
        txt = -0.000190561 + 0.886117 * jax.random.normal(jax.random.fold_in(_rk, 2), (2, 128, 192), jnp.float32)
        return (x, txt)
    x, txt = _rec_inputs()

    def _L0_tok_setup():
        import jax, jax.numpy as jnp
        import numpy as np
        B = 16
        IMG = 64
        CH = 3
        EMBED = 64
        GP = 16
        PRE = [1, 2, 4]
        N_LEVELS = 3
        FUSED = EMBED * N_LEVELS

        def hilbert_flat_indices(n):
            t = np.arange(n * n, dtype=np.int64)
            x = np.zeros(n * n, dtype=np.int64)
            y = np.zeros(n * n, dtype=np.int64)
            s = 1
            while s < n:
                rx = 1 & t // 2
                ry = 1 & (t ^ rx)
                swap = ry == 0
                flip = swap & (rx == 1)
                x = np.where(flip, s - 1 - x, x)
                y = np.where(flip, s - 1 - y, y)
                x2 = np.where(swap, y, x)
                y2 = np.where(swap, x, y)
                x, y = (x2, y2)
                x = x + s * rx
                y = y + s * ry
                t = t // 4
                s *= 2
            return y * n + x

        def _level(x, idx, W, b, p, gp):
            Bsz, C, H, _ = x.shape
            h = H // p
            t = x.reshape(Bsz, C, h, p, h, p).transpose(0, 2, 4, 3, 5, 1).reshape(Bsz, h * h, p * p * C)
            t = t[:, idx]
            t = t.reshape(Bsz, h * h // gp, gp * p * p * C)
            return t @ W.T + b

        def _interp_linear(x, n_out):
            L = x.shape[1]
            pos = (jnp.arange(n_out, dtype=jnp.float32) + 0.5) * (L / n_out) - 0.5
            pos = jnp.clip(pos, 0.0, L - 1)
            i0 = jnp.floor(pos).astype(jnp.int32)
            i1 = jnp.minimum(i0 + 1, L - 1)
            w = (pos - i0).astype(x.dtype)
            return x[:, i0] * (1.0 - w)[None, :, None] + x[:, i1] * w[None, :, None]
        key = jax.random.key(seed)
        ks = jax.random.split(key, 9)
        inp = {'x': jax.random.normal(ks[0], (B, CH, IMG, IMG), jnp.float32)}
        for i, p in enumerate(PRE):
            din = CH * p * p * GP
            inp[f'W{i}'] = jax.random.normal(ks[1 + 2 * i], (EMBED, din), jnp.float32) * din ** (-0.5)
            inp[f'b{i}'] = jax.random.normal(ks[2 + 2 * i], (EMBED,), jnp.float32) * 0.02
        inp['Wf'] = jax.random.normal(ks[7], (FUSED, FUSED), jnp.float32) * FUSED ** (-0.5)
        inp['bf'] = jax.random.normal(ks[8], (FUSED,), jnp.float32) * 0.02
        for i, p in enumerate(PRE):
            inp[f'idx{i}'] = jnp.asarray(hilbert_flat_indices(IMG // p), jnp.int32)
        return inp
    _L0_tok_all = _L0_tok_setup()
    _L0_tok_in = {k: v for k, v in _L0_tok_all.items() if k in ('W0', 'b0', 'W1', 'b1', 'W2', 'b2', 'Wf', 'bf', 'idx0', 'idx1', 'idx2')}
    del _L0_tok_all

    def _L0_attn_setup():
        import jax, jax.numpy as jnp
        import numpy as np
        B, S, D = (4, 512, 192)
        H = 12
        HD = D // H
        SCALE = HD ** (-0.5)
        key = jax.random.key(seed)
        ks = jax.random.split(key, 5)
        x = jax.random.normal(ks[0], (B, S, D), dtype=jnp.float32)
        w_qkv = jax.random.normal(ks[1], (D, 3 * D), dtype=jnp.float32) * D ** (-0.5)
        b_qkv = jax.random.normal(ks[2], (3 * D,), dtype=jnp.float32) * 0.02
        w_out = jax.random.normal(ks[3], (D, D), dtype=jnp.float32) * D ** (-0.5)
        b_out = jax.random.normal(ks[4], (D,), dtype=jnp.float32) * 0.02
        return {'x': x, 'w_qkv': w_qkv, 'b_qkv': b_qkv, 'w_out': w_out, 'b_out': b_out}
    _L0_attn_all = _L0_attn_setup()
    _L0_attn_in = {k: v for k, v in _L0_attn_all.items() if k in ('w_qkv', 'b_qkv', 'w_out', 'b_out')}
    del _L0_attn_all

    def _L0_ffn_setup():
        import jax, jax.numpy as jnp
        import numpy as np
        DIM = 192
        NUM_EXPERTS = 4
        NUM_HEADS = 12
        HEAD_DIM = DIM // NUM_HEADS
        MLP_HID = 4 * DIM
        FC1_OUT = MLP_HID + 3 * DIM
        FC2_IN = MLP_HID + DIM
        FC2_OUT = 2 * DIM
        CAP_FACTOR = 0.5
        LN_EPS = 1e-06
        key = jax.random.key(seed)
        ks = jax.random.split(key, 4)
        B, N = (8, 256)
        return {'x': jax.random.normal(ks[0], (B, N, DIM), jnp.float32), 'w_router': jax.random.normal(ks[1], (NUM_EXPERTS, DIM), jnp.float32) * 0.02, 'gamma1': jnp.ones((DIM,), jnp.float32), 'beta1': jnp.zeros((DIM,), jnp.float32), 'w1': jax.random.normal(ks[2], (FC1_OUT, DIM), jnp.float32) * 0.02, 'b1': jnp.zeros((FC1_OUT,), jnp.float32), 'w2': jax.random.normal(ks[3], (FC2_OUT, FC2_IN), jnp.float32) * 0.02, 'b2': jnp.zeros((FC2_OUT,), jnp.float32)}
    _L0_ffn_all = _L0_ffn_setup()
    _L0_ffn_in = {k: v for k, v in _L0_ffn_all.items() if k in ('w_router', 'gamma1', 'beta1', 'w1', 'b1', 'w2', 'b2')}
    del _L0_ffn_all
    return {'x': x, 'txt': txt, 'L0_tok_W0': _L0_tok_in['W0'], 'L0_tok_b0': _L0_tok_in['b0'], 'L0_tok_W1': _L0_tok_in['W1'], 'L0_tok_b1': _L0_tok_in['b1'], 'L0_tok_W2': _L0_tok_in['W2'], 'L0_tok_b2': _L0_tok_in['b2'], 'L0_tok_Wf': _L0_tok_in['Wf'], 'L0_tok_bf': _L0_tok_in['bf'], 'L0_tok_idx0': _L0_tok_in['idx0'], 'L0_tok_idx1': _L0_tok_in['idx1'], 'L0_tok_idx2': _L0_tok_in['idx2'], 'L0_attn_w_qkv': _L0_attn_in['w_qkv'], 'L0_attn_b_qkv': _L0_attn_in['b_qkv'], 'L0_attn_w_out': _L0_attn_in['w_out'], 'L0_attn_b_out': _L0_attn_in['b_out'], 'L0_ffn_w_router': _L0_ffn_in['w_router'], 'L0_ffn_gamma1': _L0_ffn_in['gamma1'], 'L0_ffn_beta1': _L0_ffn_in['beta1'], 'L0_ffn_w1': _L0_ffn_in['w1'], 'L0_ffn_b1': _L0_ffn_in['b1'], 'L0_ffn_w2': _L0_ffn_in['w2'], 'L0_ffn_b2': _L0_ffn_in['b2']}

def reference(x, txt, L0_tok_W0, L0_tok_b0, L0_tok_W1, L0_tok_b1, L0_tok_W2, L0_tok_b2, L0_tok_Wf, L0_tok_bf, L0_tok_idx0, L0_tok_idx1, L0_tok_idx2, L0_attn_w_qkv, L0_attn_b_qkv, L0_attn_w_out, L0_attn_b_out, L0_ffn_w_router, L0_ffn_gamma1, L0_ffn_beta1, L0_ffn_w1, L0_ffn_b1, L0_ffn_w2, L0_ffn_b2):
    import jax
    import jax.numpy as jnp

    def _L0_tok_ref(x, W0, b0, W1, b1, W2, b2, Wf, bf, idx0, idx1, idx2):
        import jax, jax.numpy as jnp
        import numpy as np
        B = 16
        IMG = 64
        CH = 3
        EMBED = 64
        GP = 16
        PRE = [1, 2, 4]
        N_LEVELS = 3
        FUSED = EMBED * N_LEVELS

        def hilbert_flat_indices(n):
            t = np.arange(n * n, dtype=np.int64)
            x = np.zeros(n * n, dtype=np.int64)
            y = np.zeros(n * n, dtype=np.int64)
            s = 1
            while s < n:
                rx = 1 & t // 2
                ry = 1 & (t ^ rx)
                swap = ry == 0
                flip = swap & (rx == 1)
                x = np.where(flip, s - 1 - x, x)
                y = np.where(flip, s - 1 - y, y)
                x2 = np.where(swap, y, x)
                y2 = np.where(swap, x, y)
                x, y = (x2, y2)
                x = x + s * rx
                y = y + s * ry
                t = t // 4
                s *= 2
            return y * n + x

        def _level(x, idx, W, b, p, gp):
            Bsz, C, H, _ = x.shape
            h = H // p
            t = x.reshape(Bsz, C, h, p, h, p).transpose(0, 2, 4, 3, 5, 1).reshape(Bsz, h * h, p * p * C)
            t = t[:, idx]
            t = t.reshape(Bsz, h * h // gp, gp * p * p * C)
            return t @ W.T + b

        def _interp_linear(x, n_out):
            L = x.shape[1]
            pos = (jnp.arange(n_out, dtype=jnp.float32) + 0.5) * (L / n_out) - 0.5
            pos = jnp.clip(pos, 0.0, L - 1)
            i0 = jnp.floor(pos).astype(jnp.int32)
            i1 = jnp.minimum(i0 + 1, L - 1)
            w = (pos - i0).astype(x.dtype)
            return x[:, i0] * (1.0 - w)[None, :, None] + x[:, i1] * w[None, :, None]
        Ws = [(idx0, W0, b0, PRE[0]), (idx1, W1, b1, PRE[1]), (idx2, W2, b2, PRE[2])]
        outs = [_level(x, idx, W, b, p, GP) for idx, W, b, p in Ws]
        n_tokens = outs[0].shape[1]
        outs = [outs[0]] + [_interp_linear(o, n_tokens) for o in outs[1:]]
        y = jnp.concatenate(outs, axis=-1)
        return y @ Wf.T + bf

    def _L0_attn_ref(x, w_qkv, b_qkv, w_out, b_out):
        import jax, jax.numpy as jnp
        import numpy as np
        B, S, D = (4, 512, 192)
        H = 12
        HD = D // H
        SCALE = HD ** (-0.5)
        b, s, _ = x.shape
        qkv = (x @ w_qkv + b_qkv).reshape(b, s, 3, H, HD)
        q, k, v = jnp.moveaxis(qkv, 2, 0)
        q = q.transpose(0, 2, 1, 3)
        k = k.transpose(0, 2, 1, 3)
        v = v.transpose(0, 2, 1, 3)
        scores = jnp.einsum('bhqd,bhkd->bhqk', q, k) * SCALE
        attn = jax.nn.softmax(scores, axis=-1)
        out = jnp.einsum('bhqk,bhkd->bhqd', attn, v)
        out = out.transpose(0, 2, 1, 3).reshape(b, s, D)
        return out @ w_out + b_out

    def _L0_ffn_ref(x, w_router, gamma1, beta1, w1, b1, w2, b2):
        import jax, jax.numpy as jnp
        import numpy as np
        DIM = 192
        NUM_EXPERTS = 4
        NUM_HEADS = 12
        HEAD_DIM = DIM // NUM_HEADS
        MLP_HID = 4 * DIM
        FC1_OUT = MLP_HID + 3 * DIM
        FC2_IN = MLP_HID + DIM
        FC2_OUT = 2 * DIM
        CAP_FACTOR = 0.5
        LN_EPS = 1e-06
        B, N, C = x.shape
        E = NUM_EXPERTS
        cap = int(CAP_FACTOR * N)
        m = np.array([C // 2 ** (E - 1 - e) for e in range(E)])
        in_mask = (np.arange(C)[None, :] < m[:, None]).astype(np.float32)
        in_mask = jnp.asarray(in_mask)
        out_mask = jnp.concatenate([in_mask, in_mask], axis=-1)
        logits = jnp.einsum('bnc,ec->bne', x, w_router)
        probs = jax.nn.softmax(logits, axis=-1)
        gate, idx = jax.lax.top_k(jnp.swapaxes(probs, 1, 2), cap)
        dispatch = jax.nn.one_hot(idx, N, dtype=x.dtype)
        combine = dispatch * gate[..., None]
        mu = jnp.mean(x, -1, keepdims=True)
        var = jnp.var(x, -1, keepdims=True)
        y = (x - mu) * jax.lax.rsqrt(var + LN_EPS) * gamma1 + beta1
        xg = jnp.einsum('becn,bnd->becd', dispatch, y)
        xg = xg * in_mask[None, :, None, :]
        h = jnp.einsum('becd,fd->becf', xg, w1) + b1
        h = jnp.einsum('becn,becf->bnf', dispatch, h)
        x_mlp, x_qkv = (h[..., :MLP_HID], h[..., MLP_HID:])
        qkv = x_qkv.reshape(B, N, 3, NUM_HEADS, HEAD_DIM).transpose(2, 0, 3, 1, 4)
        q, k, v = (qkv[0], qkv[1], qkv[2])
        scale = HEAD_DIM ** (-0.5)
        attn = jax.nn.softmax(jnp.einsum('bhqd,bhkd->bhqk', q, k) * scale, axis=-1)
        x_attn = jnp.einsum('bhqk,bhkd->bhqd', attn, v)
        x_attn = x_attn.transpose(0, 2, 1, 3).reshape(B, N, C)
        x_mlp = jax.nn.gelu(x_mlp, approximate=False)
        y2 = jnp.concatenate([x_mlp, x_attn], axis=-1)
        yg = jnp.einsum('becn,bnf->becf', dispatch, y2)
        o = jnp.einsum('becf,of->beco', yg, w2) + b2
        o = o * out_mask[None, :, None, :]
        z = jnp.einsum('becn,beco->bno', combine, o)
        x_mlp2, x_attn2 = (z[..., :C], z[..., C:])
        return x + x_mlp2 + x_attn2
    h = _L0_tok_ref(x, L0_tok_W0, L0_tok_b0, L0_tok_W1, L0_tok_b1, L0_tok_W2, L0_tok_b2, L0_tok_Wf, L0_tok_bf, L0_tok_idx0, L0_tok_idx1, L0_tok_idx2)
    h = jnp.concatenate([h, txt], axis=1)
    h = h + _L0_attn_ref(_layernorm(h, axis=-1), L0_attn_w_qkv, L0_attn_b_qkv, L0_attn_w_out, L0_attn_b_out)
    h = h + _L0_ffn_ref(_layernorm(h, axis=-1), L0_ffn_w_router, L0_ffn_gamma1, L0_ffn_beta1, L0_ffn_w1, L0_ffn_b1, L0_ffn_w2, L0_ffn_b2)
    return h

_drawn_inputs = setup_inputs


def setup_inputs(seed=0):
    import zlib

    import numpy as np

    out = dict(_drawn_inputs(seed))
    spreads = {'L0_ffn_gamma1': (1.0, 0.6),
     'L0_ffn_beta1': (0.0, 0.8),
     'L0_ffn_b1': (0.0, 0.324),
     'L0_ffn_b2': (0.0, 0.319)}
    factors = {'L0_tok_b0': 4.191, 'L0_tok_b1': 4.338, 'L0_tok_b2': 3.336}
    for name, (base, spread) in spreads.items():
        noise = np.random.default_rng([zlib.crc32(name.encode()), seed]).standard_normal(out[name].shape)
        drawn = base * np.exp(spread * noise) if base else spread * noise
        out[name] = jnp.asarray(drawn.astype(out[name].dtype))
    for name, factor in factors.items():
        out[name] = (out[name] * factor).astype(out[name].dtype)
    return out
```

```python
from contextlib import ExitStack

import numpy as np

import concourse.bass as bass
from concourse import mybir

F32 = mybir.dt.float32
F32R = mybir.dt.float32r
BF16 = mybir.dt.bfloat16
U32 = mybir.dt.uint32
ALU = mybir.AluOpType
ACT = mybir.ActivationFunctionType
AX_X = mybir.AxisListType.X

P = 128
B = 2
IMG = 64
CH = 3
GP = 16
EMBED = 64
D = 192
D2 = D - P
IMG_TOK = 256
TXT_TOK = 128
SEQ = IMG_TOK + TXT_TOK
TOK = B * SEQ
NT = TOK // P
TB = SEQ // P
H = 12
HD = D // H
SLOT = 64
PAIRS = H // 2
HEADS = B * H
GROUP = 3
GROUPS = HEADS // GROUP
AHEAD = 6
VW = HD + 1
MLP = 4 * D
MT = MLP // P
E = 4
CAP = SEQ // 2
BLOCKS = [0, 24, 48, 96, 192]
KC = MT + 2


def constants():
    def interp(n_in):
        pos = np.clip((np.arange(IMG_TOK) + 0.5) * (n_in / IMG_TOK) - 0.5, 0, n_in - 1)
        i0 = np.floor(pos).astype(int)
        i1 = np.minimum(i0 + 1, n_in - 1)
        w = pos - i0
        a = np.zeros((B, n_in, B, IMG_TOK), np.float32)
        for b in range(B):
            a[b, i0, b, np.arange(IMG_TOK)] += (1.0 - w).astype(np.float32)
            a[b, i1, b, np.arange(IMG_TOK)] += w.astype(np.float32)
        return a.reshape(B * n_in, B * IMG_TOK)

    wide = np.zeros((P, P + 512 + 16), np.float32)
    wide[:, :P] = np.eye(P)
    wide[:, P:P + 512] = interp(64)
    wide[:, P + 512 + 7] = 1.0
    small = np.zeros((32, 512 + E * P + B * (D + 1)), np.float32)
    small[:, :512] = interp(16)
    for e in range(E):
        small[[e, E + e, 2 * E + e], 512 + e * P:512 + (e + 1) * P] = 1.0
    for b in range(B):
        at = 512 + E * P + b * (D + 1)
        for e in range(E):
            small[b * E + e, at:at + BLOCKS[e + 1]] = 1.0
            small[b * E + e, at + D] = 1.0
    return wide, small


def ring_uses():
    uses = []
    for step in range(-AHEAD, HEADS + 1):
        head = step + AHEAD
        if head < HEADS:
            uses += [("S", head, qt) for qt in range(TB)]
        if 0 < head <= HEADS and head % GROUP == 0:
            uses.append(("M", head // GROUP - 1))
    return uses


def early_fusion(nc, rows0, rows1, rows2, idx0, idx1, idx2, w0, w1, w2, tok_bias, wf, bf, txt,
                 wqkv, wout, wr, gb, fc1, fc2, wide, small, out):
    uses = ring_uses()
    use_at = {u: n for n, u in enumerate(uses)}
    with ExitStack() as ctx:
        def sb(name, shape, dt=F32):
            return ctx.enter_context(nc.sbuf_tensor(name, shape, dt))

        def sem(name):
            return ctx.enter_context(nc.semaphore(name))

        psum = ctx.enter_context(nc.psum_tensor("psum", [P, 8, 512], F32))

        wide_sb = sb("wide_sb", [P, P + 512 + 16])
        small_sb = sb("small_sb", [32, 512 + E * P + B * (D + 1)])
        eye = wide_sb[:, 0:P]
        interp1 = wide_sb[:, P:P + 512]
        interp2 = small_sb[:, 0:512]
        eye_bf = sb("eye_bf", [P, P], BF16)
        pick_col = sb("pick_col", [P, 15], BF16)
        spread = sb("spread", [3 * E, E, P], BF16)
        masks = small_sb[0:B * E, 512 + E * P:].rearrange("p (b d) -> p b d", b=B)
        ix0 = sb("ix0", [P, 32], U32)
        ix1 = sb("ix1", [P, 8], U32)
        ix2 = sb("ix2", [P, 2], U32)
        w0_sb = sb("w0_sb", [48, EMBED])
        w1_sb = sb("w1_sb", [96, 2, EMBED])
        w2_sb = sb("w2_sb", [96, 8, EMBED])
        tok_bias_sb = sb("tok_bias_sb", [EMBED, 3])
        wf_sb = sb("wf_sb", [EMBED, 3, D])
        bf_sb = sb("bf_sb", [P, D])
        wqkv_a = sb("wqkv_a", [P, 3 * D])
        wqkv_b = sb("wqkv_b", [D2 + 1, 3 * D])
        wout_a = sb("wout_a", [P, D])
        wout_b = sb("wout_b", [D2 + 1, D])
        wr_a = sb("wr_a", [P, E])
        wr_b = sb("wr_b", [D2, E])
        gb_a = sb("gb_a", [P, 2])
        gb_b = sb("gb_b", [D2, 2])
        fc1_a = sb("fc1_a", [P, MLP + 3 * D])
        fc1_b = sb("fc1_b", [D2 + 1, MLP + 3 * D])
        fc2_in = sb("fc2_in", [P, KC, 2 * D])
        fc2_sb = fc2_in[:, :, 0:D]

        gat0 = sb("gat0", [P, 32, 6])
        gat1 = sb("gat1", [P, 8, 24])
        gat2 = sb("gat2", [P, 2, 96])
        turned0 = sb("turned0", [48, 512])
        own0 = sb("own0", [P, 2, B, GP, CH])
        own1 = sb("own1", [P, B, 8, 12])
        own2 = sb("own2", [P, B, 2, 48])
        turned1 = sb("turned1", [96, 2, B, 64])
        turned2 = sb("turned2", [96, 8, B, 16])
        level1 = sb("level1", [P, EMBED])
        level2 = sb("level2", [32, EMBED])
        levels = sb("levels", [EMBED, 3, 512])

        hid = sb("hid", [P, NT, D])
        xn = sb("xn", [P, NT, D])
        stats = sb("stats", [P, NT, 6])
        mv = sb("mv", [P, NT, 2])
        var_eps = sb("var_eps", [P, NT])
        rstd = sb("rstd", [P, NT])
        half = sb("half", [P, NT])
        x_a = sb("x_a", [P, TOK])
        x_b = sb("x_b", [D2 + 1, TOK])
        nat_q = sb("nat_q", [P, 2, H, SLOT])
        nat_k = sb("nat_k", [P, 2, H, SLOT])
        q_t = sb("q_t", [P, PAIRS, TOK], F32R)
        k_t = sb("k_t", [P, PAIRS, TOK], F32R)
        v_sb = sb("v_sb", [P, NT, H, VW])
        neg_max = sb("neg_max", [P, 3, TB, GROUP])
        max_row = sb("max_row", [GROUP, 2, SEQ], F32R)
        prob = sb("prob", [P, 3, TB, SEQ])
        den = sb("den", [P, 2, GROUP * TB])
        att = sb("att", [P, NT, D])
        att_a = sb("att_a", [P, TOK])
        att_b = sb("att_b", [D2 + 1, TOK])

        y0 = sb("y0", [P, NT, D])
        xf_a, xf_b = att_a, att_b
        top = sb("top", [P, NT])
        gate = sb("gate", [P, NT, E])
        gsum = sb("gsum", [P, NT])
        part = sb("part", [P, NT, 3, E], BF16)
        rest = sb("rest", [P, NT, 2, E])
        gate_rows = sb("gate_rows", [3 * E, NT, P], BF16)
        beats = sb("beats", [P, 4, SEQ], BF16)
        ones_row = sb("ones_row", [B * E, SEQ])
        rank = sb("rank", [B * E, SEQ])
        inside = sb("inside", [B * E, SEQ])
        last_rank = sb("last_rank", [B * E, 1])
        room = sb("room", [B * E, 1])
        at_edge = sb("at_edge", [B * E, SEQ])
        place = sb("place", [B * E, SEQ])
        chosen = sb("chosen", [B * E, SEQ])
        weight = sb("weight", [P, NT, E])
        weight_d = sb("weight_d", [P, NT, D])
        acc = sb("acc", [P, NT, D])
        gelu = sb("gelu", [P, MT, TOK])
        gate_all = gelu[:, 0:E, :].rearrange("p c (b n) -> p b c n", b=B)
        z = y0

        in_idx = sem("in_idx")
        in_tok = sem("in_tok")
        in_txt = sem("in_txt")
        in_qkv = sem("in_qkv")
        in_out = sem("in_out")
        in_fc1 = sem("in_fc1")
        in_fc2 = sem("in_fc2")
        got1 = sem("got1")
        got2 = sem("got2")
        got0 = sem("got0")
        consts_ready = sem("consts_ready")
        apart = sem("apart")
        pe_tok = sem("pe_tok")
        ev_tok = sem("ev_tok")
        ev_level = sem("ev_level")
        dve_done = sem("dve_done")
        act_done = sem("act_done")
        mv_ready = sem("mv_ready")
        rstd_ready = sem("rstd_ready")
        xn_ready = sem("xn_ready")
        pe_turn = sem("pe_turn")
        turned = sem("turned")
        qkv_done = sem("qkv_done")
        high_ready = sem("high_ready")
        low_ready = sem("low_ready")
        stack_psum = sem("stack_psum")
        stack_ready = sem("stack_ready")
        s1_done = sem("s1_done")
        max_ready = sem("max_ready")
        rows_psum = sem("rows_psum")
        rows_ready = sem("rows_ready")
        rows_in = [[sem(f"rows_in_{n}_{layer}") for n in range(GROUPS)] for layer in range(2)]
        s2_done = sem("s2_done")
        exp_ready = sem("exp_ready")
        av_done = sem("av_done")
        norm_ready = sem("norm_ready")
        proj_done = sem("proj_done")
        hid_ready = sem("hid_ready")
        logits_done = sem("logits_done")
        logits_in = sem("logits_in")
        exp4_ready = sem("exp4_ready")
        parts_ready = sem("parts_ready")
        parts_psum = sem("parts_psum")
        gate_rows_ready = sem("gate_rows_ready")
        spread_done = sem("spread_done")
        gate_all_ready = sem("gate_all_ready")
        beats_ready = sem("beats_ready")
        rank_done = sem("rank_done")
        counted = sem("counted")
        chosen_ready = sem("chosen_ready")
        chosen_psum = sem("chosen_psum")
        coef_psum = sem("coef_psum")
        hin_ready = sem("hin_ready")
        fc1_done = sem("fc1_done")
        gelu_ready = sem("gelu_ready")
        fc2_done = sem("fc2_done")
        z_ready = sem("z_ready")
        stored = sem("stored")

        block = ctx.enter_context(nc.Block())

        def s1_count(layer, head, qt):
            return layer * HEADS * TB + head * TB + qt + 1

        @block.sync
        def _(sp):
            sp.dma_start(ix1[:], idx1).then_inc(in_idx, 16)
            sp.dma_start(ix2[:], idx2).then_inc(in_idx, 16)
            sp.dma_start(ix0[:], idx0).then_inc(in_idx, 16)
            for dst, src in ((wide_sb, wide), (small_sb, small), (w1_sb, w1), (w2_sb, w2), (w0_sb, w0),
                             (tok_bias_sb, tok_bias), (wf_sb, wf)):
                sp.dma_start(dst[:], src).then_inc(in_tok, 16)
            sp.dma_start(bf_sb[:], bf[0:1, :].to_broadcast([P, D])).then_inc(in_tok, 16)
            for b in range(B):
                sp.dma_start(hid[:, TB * b + TB - 1, :], txt[b]).then_inc(in_txt, 16)
            sp.dma_start(wqkv_a[:], wqkv[0:P]).then_inc(in_qkv, 16)
            sp.dma_start(wqkv_b[:], wqkv[P:]).then_inc(in_qkv, 16)
            sp.dma_start(wout_a[:], wout[0:P]).then_inc(in_out, 16)
            sp.dma_start(wout_b[:], wout[P:]).then_inc(in_out, 16)
            sp.dma_start(wr_a[:], wr[0:P]).then_inc(in_out, 16)
            sp.dma_start(wr_b[:], wr[P:]).then_inc(in_out, 16)
            sp.dma_start(gb_a[:], gb[0:P]).then_inc(in_out, 16)
            sp.dma_start(gb_b[:], gb[P:]).then_inc(in_out, 16)
            sp.dma_start(fc1_a[:], fc1[0:P]).then_inc(in_fc1, 16)
            sp.dma_start(fc1_b[:], fc1[P:]).then_inc(in_fc1, 16)
            sp.dma_start(fc2_in[:, 0:KC - 1, :], fc2[0:(KC - 1) * P].rearrange("(c p) d -> p c d", p=P)).then_inc(in_fc2, 16)
            sp.dma_start(fc2_in[0:D2 + 1, KC - 1, :], fc2[(KC - 1) * P:]).then_inc(in_fc2, 16)

            for layer in range(2):
                for g in range(GROUPS):
                    sp.wait_ge(rows_ready, layer * GROUPS + g + 1)
                    for n in range(GROUP):
                        b, h = divmod(g * GROUP + n, H)
                        at = SLOT * (h % 2) + 3 * HD
                        sp.dma_start(q_t[at:at + 1, h // 2, b * SEQ:(b + 1) * SEQ].bitcast(F32),
                                     max_row[n:n + 1, g % 2, :].bitcast(F32)).then_inc(rows_in[layer][g], 16)
            for t in range(NT):
                b, p = divmod(t, TB)
                sp.wait_ge(z_ready, t + 1)
                sp.dma_start(out[b, p * P:(p + 1) * P, :], z[:, t, :]).then_inc(stored, 16)
            sp.wait_ge(stored, 16 * NT)

        @block.gpsimd
        def _(pool):
            pool.wait_ge(in_idx, 48)

            def gather(dst, rows, index, done):
                nc.gpsimd.indirect_dma_start(
                    out=dst, out_offset=None, in_=rows,
                    in_offset=bass.IndirectOffsetOnAxis(ap=index, axis=0)).then_inc(done, 16)

            for j in range(8):
                gather(gat1[:, j, :], rows1, ix1[:, j:j + 1], got1)
            for j in range(2):
                gather(gat2[:, j, :], rows2, ix2[:, j:j + 1], got2)
            for j in range(32):
                gather(gat0[:, j, :], rows0, ix0[:, j:j + 1], got0)

            pool.wait_ge(consts_ready, 1)
            for n in range(3):
                pool.wait_ge(mv_ready, n + 1)
                pool.tensor_tensor(rstd[:], var_eps[:], half[:], ALU.pow).then_inc(rstd_ready, 1)

        @block.tensor
        def _(pe):
            mm = nc.tensor.matmul

            pe.wait_ge(in_tok, 128)
            pe.wait_ge(apart, 1)
            for b in range(B):
                last = nc.tensor.transpose(psum[0:96, 0, b * P:(b + 1) * P], own1[:, b].rearrange("p j c -> p (j c)"), eye)
            last.then_inc(pe_tok, 1)
            pe.wait_ge(apart, 2)
            for b in range(B):
                last = nc.tensor.transpose(psum[0:96, 1, b * P:(b + 1) * P], own2[:, b].rearrange("p j c -> p (j c)"), eye)
            last.then_inc(pe_tok, 1)
            pe.wait_ge(ev_tok, 1)
            for jh in range(2):
                last = mm(psum[:, 2, 0:EMBED], turned1[:, jh].rearrange("p b g -> p (b g)"), w1_sb[:, jh, :],
                          start=jh == 0, stop=jh == 1)
            last.then_inc(pe_tok, 1)
            pe.wait_ge(ev_tok, 2)
            for jh in range(8):
                last = mm(psum[0:32, 3, 0:EMBED], turned2[:, jh].rearrange("p b g -> p (b g)"), w2_sb[:, jh, :],
                          start=jh == 0, stop=jh == 7)
            last.then_inc(pe_tok, 1)
            pe.wait_ge(ev_tok, 3)
            mm(psum[0:EMBED, 4, :], level1[:], interp1, start=True, stop=True).then_inc(pe_tok, 1)
            pe.wait_ge(ev_tok, 4)
            mm(psum[0:EMBED, 5, :], level2[:], interp2, start=True, stop=True).then_inc(pe_tok, 1)
            pe.wait_ge(apart, 3)
            for n in range(4):
                b, gt = divmod(n, 2)
                last = nc.tensor.transpose(psum[0:48, 6, n * P:(n + 1) * P],
                                           own0[:, gt, b].rearrange("p j c -> p (j c)"), eye)
            last.then_inc(pe_tok, 1)
            pe.wait_ge(ev_level, 3)
            mm(psum[0:EMBED, 7, :], w0_sb[:], turned0[:], start=True, stop=True).then_inc(pe_tok, 1)
            pe.wait_ge(ev_level, 4)
            for n in range(4):
                for lv in range(3):
                    last = mm(psum[:, n, 0:D], levels[:, lv, n * P:(n + 1) * P], wf_sb[:, lv, :],
                              start=lv == 0, stop=lv == 2)
                last.then_inc(pe_tok, 1)

            def turn(src, t, bank, done):
                nc.tensor.transpose(psum[:, bank, 0:P], src[:, t, 0:P], eye)
                nc.tensor.transpose(psum[0:D2, bank, P:2 * P], src[:, t, P:D], eye).then_inc(done, 1)

            def project(layer, weights, at):
                wa, wb = weights

                def stacks(t):
                    pe.wait_ge(high_ready, 2 * (layer * NT + t + 1))
                    pe.wait_ge(low_ready, layer * NT + t + 1)
                    for u in range(3):
                        n = 3 * (layer * NT + t) + u
                        if n >= 2:
                            pe.wait_ge(stack_ready, n - 1)
                        for i in range(4):
                            c = 4 * u + i
                            nat = (nat_q, nat_k)[c // PAIRS]
                            pair = c % PAIRS
                            last = nc.tensor.transpose(
                                psum[:, 6 + n % 2, i * P:(i + 1) * P],
                                nat[:, t % 2, 2 * pair:2 * pair + 2, :], eye)
                        last.then_inc(stack_psum, 1)

                for t in range(NT):
                    if layer == 0:
                        pe.wait_ge(xn_ready, t + 1)
                        if t >= 2:
                            pe.wait_ge(turned, t - 1)
                        turn(xn, t, 4 + t % 2, pe_turn)
                        pe.wait_ge(turned, t + 1)
                    else:
                        pe.wait_ge(hin_ready, t // TB + 1)
                    if t >= 2:
                        pe.wait_ge(high_ready, 2 * (layer * NT + t - 1))
                        pe.wait_ge(low_ready, layer * NT + t - 1)
                    tok = slice(t * P, (t + 1) * P)
                    for bank, w in ((2 * (t % 2), slice(at, at + 2 * D)),
                                    (2 * (t % 2) + 1, slice(at + 2 * D, at + 3 * D))):
                        n = w.stop - w.start
                        mm(psum[:, bank, 0:n], x_a[:, tok], wa[:, w], start=True, stop=False)
                        last = mm(psum[:, bank, 0:n], x_b[:, tok], wb[:, w], start=False, stop=True)
                    last.then_inc(qkv_done, 1)
                    if t >= 1:
                        stacks(t - 1)
                stacks(NT - 1)

            def attention(layer):
                def free_ring_bank(n):
                    if n < 2:
                        return
                    if uses[n - 2][0] == "S":
                        pe.wait_ge(max_ready, s1_count(layer, uses[n - 2][1], uses[n - 2][2]))
                    else:
                        pe.wait_ge(rows_ready, layer * GROUPS + uses[n - 2][1] + 1)

                def scores_for_max(head):
                    b, h = divmod(head, H)
                    rows = slice(SLOT * (h % 2), SLOT * (h % 2) + 3 * HD)
                    for qt in range(TB):
                        n = use_at[("S", head, qt)]
                        free_ring_bank(n)
                        mm(psum[:, n % 2, 0:SEQ], q_t[rows, h // 2, b * SEQ + qt * P:b * SEQ + (qt + 1) * P],
                           k_t[rows, h // 2, b * SEQ:(b + 1) * SEQ], start=True, stop=True).then_inc(s1_done, 1)

                def turn_maxima(g):
                    n = use_at[("M", g)]
                    free_ring_bank(n)
                    pe.wait_ge(max_ready, s1_count(layer, g * GROUP + GROUP - 1, TB - 1))
                    for qt in range(TB):
                        last = nc.tensor.transpose(psum[0:GROUP, n % 2, qt * P:(qt + 1) * P],
                                                   neg_max[:, g % 3, qt, :], eye)
                    last.then_inc(rows_psum, 1)

                def scores_for_exp(head):
                    b, h = divmod(head, H)
                    rows = slice(SLOT * (h % 2), SLOT * (h % 2) + 3 * HD + 1)
                    if head % GROUP == 0:
                        pe.wait_ge(rows_in[layer][head // GROUP], 16 * GROUP)
                    for kt in range(TB):
                        n = layer * HEADS * TB + head * TB + kt
                        if n >= 4:
                            pe.wait_ge(exp_ready, n - 3)
                        mm(psum[:, 2 + n % 4, 0:SEQ], k_t[rows, h // 2, b * SEQ + kt * P:b * SEQ + (kt + 1) * P],
                           q_t[rows, h // 2, b * SEQ:(b + 1) * SEQ], start=True, stop=True).then_inc(s2_done, 1)

                def weigh_values(head):
                    b, h = divmod(head, H)
                    g, hl = divmod(head, GROUP)
                    if hl == 0 and g >= 2:
                        pe.wait_ge(norm_ready, layer * GROUPS + g - 1)
                    pe.wait_ge(exp_ready, s1_count(layer, head, TB - 1))
                    for qt in range(TB):
                        at = (hl * TB + qt) * VW
                        for kt in range(TB):
                            last = mm(psum[:, 6 + g % 2, at:at + VW], prob[:, head % 3, kt, qt * P:(qt + 1) * P],
                                      v_sb[:, TB * b + kt, h, :], start=kt == 0, stop=kt == TB - 1)
                    last.then_inc(av_done, 1)

                pe.wait_ge(stack_ready, 3 * NT * (layer + 1))
                for step in range(-AHEAD, HEADS + 1):
                    if 0 <= step < HEADS:
                        scores_for_exp(step)
                    head = step + AHEAD
                    if head < HEADS:
                        scores_for_max(head)
                    if 0 < head <= HEADS and head % GROUP == 0:
                        turn_maxima(head // GROUP - 1)
                    if step >= 1:
                        weigh_values(step - 1)

            pe.wait_ge(in_qkv, 32)
            project(0, (wqkv_a, wqkv_b), 0)
            attention(0)

            pe.wait_ge(in_out, 96)
            for t in range(NT):
                pe.wait_ge(norm_ready, GROUPS // B * (t // TB + 1))
                if t >= 2:
                    pe.wait_ge(turned, NT + t - 1)
                turn(att, t, t % 2, pe_turn)
                pe.wait_ge(turned, NT + t + 1)
                if t >= 2:
                    pe.wait_ge(hid_ready, t - 1)
                tok = slice(t * P, (t + 1) * P)
                mm(psum[:, 2 + t % 2, 0:D], att_a[:, tok], wout_a[:], start=True, stop=False)
                mm(psum[:, 2 + t % 2, 0:D], att_b[:, tok], wout_b[:], start=False, stop=True).then_inc(proj_done, 1)

            for t in range(NT):
                pe.wait_ge(xn_ready, NT + t + 1)
                if t >= 2:
                    pe.wait_ge(turned, 2 * NT + t - 1)
                turn(xn, t, 4 + t % 2, pe_turn)
            for t in range(NT):
                pe.wait_ge(turned, 2 * NT + t + 1)
                tok = slice(t * P, (t + 1) * P)
                mm(psum[:, 6, t * E:(t + 1) * E], xf_a[:, tok], wr_a[:], start=True, stop=False)
                last = mm(psum[:, 6, t * E:(t + 1) * E], xf_b[0:D2, tok], wr_b[:], start=False, stop=True)
            last.then_inc(logits_done, 1)
            for t in range(NT):
                pe.wait_ge(xn_ready, 2 * NT + t + 1)
                if t >= 2:
                    pe.wait_ge(turned, 3 * NT + t - 1)
                turn(y0, t, 4 + t % 2, pe_turn)
            pe.wait_ge(parts_ready, 1)
            for t in range(NT):
                last = nc.tensor.transpose(
                    psum[0:3 * E, 7, t * (P // 2):(t + 1) * (P // 2)].bitcast(BF16),
                    part[:, t].rearrange("p a e -> p (a e)"), eye_bf[:])
            last.then_inc(parts_psum, 1)
            pe.wait_ge(gate_rows_ready, 1)
            for b in range(B):
                for e in range(E):
                    n = b * E + e
                    if n >= 4:
                        pe.wait_ge(gate_all_ready, n - 3)
                    mm(psum[:, n % 4, 0:SEQ], spread[:, e, :], gate_rows[:, TB * b:TB * (b + 1), :],
                       start=True, stop=True).then_inc(spread_done, 1)
            for n in range(B * E * TB):
                pe.wait_ge(beats_ready, n + 1)
                be = n // TB
                mm(psum[0:B * E, 6, 0:SEQ], pick_col[:, 7 - be:15 - be], beats[:, n % 4, :],
                   start=n == 0, stop=n == B * E * TB - 1).then_inc(counted, 1)
            pe.wait_ge(chosen_ready, 1)
            for b in range(B):
                mm(psum[:, b, 0:SEQ], masks[:, b, 0:P], chosen[:], start=True, stop=True)
                mm(psum[0:D2 + 1, 2 + b, 0:SEQ], masks[:, b, P:D + 1], chosen[:],
                   start=True, stop=True).then_inc(coef_psum, 1)
            for p in range(TB):
                last = nc.tensor.transpose(psum[:, 6, p * B * E:(p + 1) * B * E], chosen[:, p * P:(p + 1) * P],
                                           eye[0:B * E, 0:B * E])
            last.then_inc(chosen_psum, 1)

            pe.wait_ge(in_fc1, 32)
            for n in range(B * MT):
                b, f = divmod(n, MT)
                pe.wait_ge(hin_ready, b + 1)
                if n >= 2:
                    pe.wait_ge(gelu_ready, n - 1)
                tok = slice(b * SEQ, (b + 1) * SEQ)
                mm(psum[:, 4 + n % 2, 0:SEQ], fc1_a[:, f * P:(f + 1) * P], x_a[:, tok], start=True, stop=False)
                mm(psum[:, 4 + n % 2, 0:SEQ], fc1_b[:, f * P:(f + 1) * P], x_b[:, tok],
                   start=False, stop=True).then_inc(fc1_done, 1)

            project(1, (fc1_a, fc1_b), MLP)
            attention(1)

            for t in range(NT):
                pe.wait_ge(norm_ready, GROUPS + GROUPS // B * (t // TB + 1))
                if t >= 2:
                    pe.wait_ge(turned, 4 * NT + t - 1)
                turn(att, t, t % 2, pe_turn)
                if t == 0:
                    pe.wait_ge(gelu_ready, B * MT)
                if t >= 2:
                    pe.wait_ge(z_ready, t - 1)
                tok = slice(t * P, (t + 1) * P)
                for c in range(MT):
                    mm(psum[:, 2 + t % 2, 0:D], gelu[:, c, tok], fc2_sb[:, c, :], start=c == 0, stop=False)
                pe.wait_ge(turned, 4 * NT + t + 1)
                mm(psum[:, 2 + t % 2, 0:D], att_a[:, tok], fc2_sb[:, MT, :], start=False, stop=False)
                mm(psum[:, 2 + t % 2, 0:D], att_b[:, tok], fc2_sb[0:D2 + 1, MT + 1, :],
                   start=False, stop=True).then_inc(fc2_done, 1)

        @block.scalar
        def _(act):
            act.wait_ge(pe_tok, 5)
            act.wait_ge(in_tok, 128)
            act.activation(levels[:, 1, :], psum[0:EMBED, 4, :], ACT.Identity, bias=tok_bias_sb[:, 1:2]).then_inc(ev_level, 1)
            act.wait_ge(pe_tok, 6)
            act.activation(levels[:, 2, :], psum[0:EMBED, 5, :], ACT.Identity, bias=tok_bias_sb[:, 2:3]).then_inc(ev_level, 1)
            act.wait_ge(pe_tok, 7)
            act.activation(turned0[:], psum[0:48, 6, :], ACT.Copy).then_inc(ev_level, 1)
            act.wait_ge(pe_tok, 8)
            act.activation(levels[:, 0, :], psum[0:EMBED, 7, :], ACT.Identity, bias=tok_bias_sb[:, 0:1]).then_inc(ev_level, 1)

            def copy_turned(n, bank, dst_a, dst_b):
                t = n % NT
                tok = slice(t * P, (t + 1) * P)
                act.wait_ge(pe_turn, n + 1)
                act.activation(dst_a[:, tok], psum[:, bank, 0:P], ACT.Copy)
                act.activation(dst_b[0:D2, tok], psum[0:D2, bank, P:2 * P], ACT.Copy).then_inc(turned, 1)

            def stacks(layer, t):
                for u in range(3):
                    n = 3 * (layer * NT + t) + u
                    act.wait_ge(stack_psum, n + 1)
                    for i0, i1 in (((0, 4),), ((0, 2), (2, 4)), ((0, 4),))[u]:
                        c = 4 * u + i0
                        dst = (q_t, k_t)[c // PAIRS]
                        pair = c % PAIRS
                        last = act.activation(
                            dst[:, pair:pair + i1 - i0, t * P:(t + 1) * P],
                            psum[:, 6 + n % 2, i0 * P:i1 * P].rearrange("p (a b) -> p a b", b=P), ACT.Copy)
                    last.then_inc(stack_ready, 1)

            def project(layer):
                for t in range(NT):
                    if layer == 0:
                        copy_turned(t, 4 + t % 2, x_a, x_b)
                    act.wait_ge(qkv_done, layer * NT + t + 1)
                    if t == 0:
                        act.wait_ge(consts_ready, 1)
                    if layer * NT + t >= 2:
                        act.wait_ge(stack_psum, 3 * (layer * NT + t - 1))
                    src = psum[:, 2 * (t % 2), 0:2 * D].rearrange("p (s h d) -> p s h d", s=2, h=H)
                    for s, nat, slots in ((0, nat_q, (0, 2)), (1, nat_k, (0, 1))):
                        dst = nat[:, t % 2].bitcast(F32R)
                        for n, slot in enumerate(slots):
                            last = act.activation(dst[:, :, slot * HD:(slot + 1) * HD], src[:, s], ACT.Copy)
                        last.then_inc(high_ready, 1)
                    if t >= 1:
                        stacks(layer, t - 1)
                stacks(layer, NT - 1)

            def attention(layer):
                for step in range(-AHEAD, HEADS + 1):
                    if 0 <= step < HEADS:
                        for kt in range(TB):
                            n = layer * HEADS * TB + step * TB + kt
                            act.wait_ge(s2_done, n + 1)
                            if layer * HEADS + step >= 3:
                                act.wait_ge(av_done, layer * HEADS + step - 2)
                            act.activation(prob[:, step % 3, kt, :], psum[:, 2 + n % 4, 0:SEQ], ACT.Exp,
                                           scale=float(HD) ** -0.5).then_inc(exp_ready, 1)
                    head = step + AHEAD
                    if 0 < head <= HEADS and head % GROUP == 0:
                        g = head // GROUP - 1
                        act.wait_ge(rows_psum, layer * GROUPS + g + 1)
                        if g >= 2:
                            act.wait_ge(rows_in[layer][g - 2], 16 * GROUP)
                        elif layer:
                            act.wait_ge(rows_in[0][GROUPS - 2 + g], 16 * GROUP)
                        act.activation(max_row[:, g % 2, :], psum[0:GROUP, use_at[("M", g)] % 2, 0:SEQ],
                                       ACT.Copy).then_inc(rows_ready, 1)

            project(0)
            attention(0)
            for t in range(NT):
                copy_turned(NT + t, t % 2, att_a, att_b)
            for t in range(NT):
                copy_turned(2 * NT + t, 4 + t % 2, xf_a, xf_b)
            act.wait_ge(logits_in, 1)
            act.activation(gate[:], gate[:], ACT.Exp).then_inc(exp4_ready, 1)
            for t in range(NT):
                tok = slice(t * P, (t + 1) * P)
                act.wait_ge(pe_turn, 3 * NT + t + 1)
                act.activation(x_a[:, tok], psum[:, 4 + t % 2, 0:P], ACT.Identity, scale=gb_a[:, 0:1], bias=gb_a[:, 1:2])
                act.activation(x_b[0:D2, tok], psum[0:D2, 4 + t % 2, P:2 * P], ACT.Identity,
                               scale=gb_b[:, 0:1], bias=gb_b[:, 1:2]).then_inc(turned, 1)
            act.wait_ge(parts_psum, 1)
            act.activation(gate_rows[:], psum[0:3 * E, 7, 0:NT * P // 2].bitcast(BF16).rearrange("p (t b) -> p t b", b=P), ACT.Copy)\
               .then_inc(gate_rows_ready, 1)
            for b in range(B):
                for e in range(E):
                    n = b * E + e
                    act.wait_ge(spread_done, n + 1)
                    act.activation(gate_all[:, b, e, :], psum[:, n % 4, 0:SEQ], ACT.Copy).then_inc(gate_all_ready, 1)
            for n in range(B * MT):
                b, f = divmod(n, MT)
                act.wait_ge(fc1_done, n + 1)
                act.activation(gelu[:, f, b * SEQ:(b + 1) * SEQ], psum[:, 4 + n % 2, 0:SEQ], ACT.Gelu).then_inc(gelu_ready, 1)
            project(1)
            attention(1)
            for t in range(NT):
                copy_turned(4 * NT + t, t % 2, att_a, att_b)

        @block.vector
        def _(dve):
            chain = [0]

            def link(instruction):
                chain[0] += 1
                instruction.then_inc(dve_done, 1)
                dve.wait_ge(dve_done, chain[0])

            dve.memset(half[:], -0.5)
            dve.memset(x_b[D2:D2 + 1, :], 1.0)
            dve.memset(att_b[D2:D2 + 1, :], 1.0)
            dve.memset(v_sb[:], 1.0)
            dve.memset(ones_row[:], 1.0)
            dve.memset(nat_q[:], 0.0)
            dve.memset(nat_k[:], 1.0).then_inc(consts_ready, 1)
            dve.wait_ge(in_tok, 128)
            dve.tensor_copy(eye_bf[:], eye)
            dve.tensor_copy(pick_col[:], wide_sb[:, P + 512:P + 512 + 15])
            link(dve.tensor_copy(spread[:], small_sb[0:3 * E, 512:512 + E * P].rearrange("p (e n) -> p e n", e=E)))
            dve.wait_ge(got1, 8 * 16)
            dve.tensor_copy(own1[:], gat1[:].rearrange("p j (b c) -> p b j c", b=B)).then_inc(apart, 1)
            dve.wait_ge(got2, 2 * 16)
            dve.tensor_copy(own2[:], gat2[:].rearrange("p j (b c) -> p b j c", b=B)).then_inc(apart, 1)
            dve.wait_ge(pe_tok, 1)
            dve.tensor_copy(turned1[:], psum[0:96, 0, 0:B * P].rearrange("p (b j g) -> p j b g", b=B, j=2)).then_inc(ev_tok, 1)
            dve.wait_ge(pe_tok, 2)
            dve.tensor_copy(turned2[:], psum[0:96, 1, 0:B * P].rearrange("p (b j g) -> p j b g", b=B, j=8)).then_inc(ev_tok, 1)
            dve.wait_ge(pe_tok, 3)
            dve.tensor_copy(level1[:], psum[:, 2, 0:EMBED]).then_inc(ev_tok, 1)
            dve.wait_ge(pe_tok, 4)
            dve.tensor_copy(level2[:], psum[0:32, 3, 0:EMBED]).then_inc(ev_tok, 1)
            dve.wait_ge(got0, 32 * 16)
            for gt in range(2):
                last = dve.tensor_copy(own0[:, gt], gat0[:, GP * gt:GP * (gt + 1), :].rearrange("p j (b c) -> p b j c", b=B))
            last.then_inc(apart, 1)
            for n in range(4):
                b, gt = divmod(n, 2)
                dve.wait_ge(pe_tok, 9 + n)
                last = dve.tensor_tensor(hid[:, TB * b + gt, :], psum[:, n, 0:D], bf_sb[:], ALU.add)
            link(last)
            dve.wait_ge(in_txt, 32)

            def layer_norm(n, src, dst, eps, ready):
                for t in range(NT):
                    last = dve.bn_stats(stats[:, t, :], src[:, t, :])
                link(last)
                for t in range(NT):
                    last = dve.bn_aggr(mv[:, t, :], stats[:, t, :])
                link(last)
                dve.tensor_scalar(var_eps[:], mv[:, :, 1], eps, None, ALU.add).then_inc(mv_ready, 1)
                dve.wait_ge(rstd_ready, n + 1)
                for t in range(NT):
                    dve.tensor_scalar(dst[:, t, :], src[:, t, :], mv[:, t, 0:1], rstd[:, t:t + 1],
                                      ALU.subtract, ALU.mult).then_inc(ready, 1)

            def project(layer):
                for t in range(NT):
                    dve.wait_ge(high_ready, 2 * (layer * NT + t + 1))
                    bank = psum[:, 2 * (t % 2), 0:2 * D].rearrange("p (s h d) -> p s h d", s=2, h=H)
                    dve.tensor_tensor(nat_q[:, t % 2, :, HD:2 * HD].bitcast(F32R), bank[:, 0], nat_q[:, t % 2, :, 0:HD], ALU.subtract)
                    dve.tensor_tensor(nat_k[:, t % 2, :, 2 * HD:3 * HD].bitcast(F32R), bank[:, 1], nat_k[:, t % 2, :, 0:HD], ALU.subtract)
                    dve.tensor_copy(v_sb[:, t, :, 0:HD], psum[:, 2 * (t % 2) + 1, 0:D].rearrange("p (h d) -> p h d", h=H))\
                       .then_inc(low_ready, 1)

            def attention(layer):
                def normalise(g):
                    b, h0 = divmod(g * GROUP, H)
                    dve.wait_ge(av_done, layer * HEADS + (g + 1) * GROUP)
                    o = psum[:, 6 + g % 2, 0:GROUP * TB * VW].rearrange("p (n d) -> p n d", d=VW)
                    link(dve.reciprocal(den[:, g % 2, :], o[:, :, HD]))
                    dst = att[:, TB * b:TB * (b + 1), h0 * HD:(h0 + GROUP) * HD].rearrange("p q (h d) -> p h q d", h=GROUP)
                    dve.tensor_tensor(dst, o[:, :, 0:HD].rearrange("p (h q) d -> p h q d", h=GROUP),
                                      den[:, g % 2, :].rearrange("p (h q o) -> p h q o", h=GROUP, o=1).to_broadcast([P, GROUP, TB, HD]),
                                      ALU.mult).then_inc(norm_ready, 1)

                for step in range(-AHEAD, HEADS + 1):
                    head = step + AHEAD
                    if head < HEADS:
                        g, hl = divmod(head, GROUP)
                        for qt in range(TB):
                            dve.wait_ge(s1_done, s1_count(layer, head, qt))
                            if hl == 0 and qt == 0 and g >= 3:
                                dve.wait_ge(rows_psum, layer * GROUPS + g - 2)
                            dve.tensor_reduce(neg_max[:, g % 3, qt, hl:hl + 1], psum[:, use_at[("S", head, qt)] % 2, 0:SEQ],
                                              AX_X, ALU.max, negate=True).then_inc(max_ready, 1)
                    if step >= 1 and step % GROUP == 0:
                        normalise(step // GROUP - 1)

            layer_norm(0, hid, xn, 1e-5, xn_ready)
            project(0)
            attention(0)

            for t in range(NT):
                dve.wait_ge(proj_done, t + 1)
                last = dve.tensor_tensor(hid[:, t, :], psum[:, 2 + t % 2, 0:D], hid[:, t, :], ALU.add)
                if t < NT - 1:
                    last.then_inc(hid_ready, 1)
            link(last)
            layer_norm(1, hid, xn, 1e-5, xn_ready)
            dve.wait_ge(xn_ready, 2 * NT)
            link(dve.tensor_tensor(acc[:], hid[:], xn[:], ALU.add))
            layer_norm(2, xn, y0, 1e-6, xn_ready)

            dve.wait_ge(logits_done, 1)
            logits = psum[:, 6, 0:NT * E].rearrange("p (t e) -> p t e", e=E)
            link(dve.tensor_reduce(top[:], logits, AX_X, ALU.max))
            dve.tensor_tensor(gate[:], logits, top[:].rearrange("p (t o) -> p t o", o=1).to_broadcast([P, NT, E]),
                              ALU.subtract).then_inc(logits_in, 1)
            dve.wait_ge(exp4_ready, 1)
            link(dve.tensor_reduce(gsum[:], gate[:], AX_X, ALU.add))
            link(dve.reciprocal(gsum[:], gsum[:]))
            link(dve.tensor_tensor(gate[:], gate[:], gsum[:].rearrange("p (t o) -> p t o", o=1).to_broadcast([P, NT, E]), ALU.mult))
            link(dve.tensor_copy(part[:, :, 0, :], gate[:]))
            link(dve.tensor_tensor(rest[:, :, 0, :], gate[:], part[:, :, 0, :], ALU.subtract))
            link(dve.tensor_copy(part[:, :, 1, :], rest[:, :, 0, :]))
            link(dve.tensor_tensor(rest[:, :, 1, :], rest[:, :, 0, :], part[:, :, 1, :], ALU.subtract))
            dve.tensor_copy(part[:, :, 2, :], rest[:, :, 1, :]).then_inc(parts_ready, 1)

            for n in range(B * E * TB):
                be, mt = divmod(n, TB)
                b, e = divmod(be, E)
                dve.wait_ge(gate_all_ready, be + 1)
                if n >= 4:
                    dve.wait_ge(counted, n - 3)
                dve.tensor_scalar(beats[:, n % 4, :], gate_all[:, b, e, :], gate[:, TB * b + mt, e:e + 1], None,
                                  ALU.is_lt).then_inc(beats_ready, 1)
            dve.wait_ge(counted, B * E * TB)
            link(dve.tensor_copy(rank[:], psum[0:B * E, 6, 0:SEQ]))
            link(dve.tensor_scalar(inside[:], rank[:], float(CAP), None, ALU.is_lt))
            link(dve.tensor_tensor(place[:], rank[:], inside[:], ALU.mult))
            link(dve.tensor_reduce(last_rank[:], place[:], AX_X, ALU.max))
            dve.tensor_scalar(room[:], last_rank[:], -1.0, float(CAP), ALU.mult, ALU.add)
            link(dve.tensor_scalar(at_edge[:], rank[:], last_rank[:, 0:1], None, ALU.is_equal))
            link(dve.tensor_tensor_scan(place[:], ones_row[:], at_edge[:], 0.0, ALU.mult, ALU.add))
            link(dve.tensor_tensor(place[:], place[:], at_edge[:], ALU.mult))
            dve.scalar_tensor_tensor(chosen[:], place[:], room[:, 0:1], inside[:], ALU.is_le, ALU.mult)\
               .then_inc(chosen_ready, 1)

            dve.wait_ge(turned, 4 * NT)
            for b in range(B):
                tok = slice(b * SEQ, (b + 1) * SEQ)
                dve.wait_ge(coef_psum, b + 1)
                dve.tensor_tensor(x_a[:, tok], x_a[:, tok], psum[:, b, 0:SEQ], ALU.mult)
                dve.tensor_tensor(x_b[:, tok], x_b[:, tok], psum[0:D2 + 1, 2 + b, 0:SEQ], ALU.mult).then_inc(hin_ready, 1)
            dve.wait_ge(chosen_psum, 1)
            for b in range(B):
                picked = psum[:, 6, 0:TB * B * E].rearrange("p (q b e) -> p q b e", b=B, e=E)[:, :, b, :]
                last = dve.tensor_tensor(weight[:, TB * b:TB * (b + 1), :], gate[:, TB * b:TB * (b + 1), :], picked, ALU.mult)
            link(last)
            for e in range(E - 2, -1, -1):
                link(dve.tensor_tensor(weight[:, :, e], weight[:, :, e], weight[:, :, e + 1], ALU.add))
            for e in range(E):
                n = BLOCKS[e + 1] - BLOCKS[e]
                dve.tensor_copy(weight_d[:, :, BLOCKS[e]:BLOCKS[e + 1]],
                                weight[:, :, e:e + 1].to_broadcast([P, NT, n]))
            dve.wait_ge(in_fc2, 32)
            dve.tensor_tensor(fc2_sb[:, 0:KC - 1, :], fc2_in[:, 0:KC - 1, 0:D], fc2_in[:, 0:KC - 1, D:2 * D], ALU.add)
            link(dve.tensor_tensor(fc2_sb[0:D2 + 1, KC - 1, :], fc2_in[0:D2 + 1, KC - 1, 0:D],
                                   fc2_in[0:D2 + 1, KC - 1, D:2 * D], ALU.add))
            project(1)
            attention(1)

            for t in range(NT):
                dve.wait_ge(fc2_done, t + 1)
                link(dve.tensor_tensor(z[:, t, :], psum[:, 2 + t % 2, 0:D], weight_d[:, t, :], ALU.mult))
                dve.tensor_tensor(z[:, t, :], z[:, t, :], acc[:, t, :], ALU.add).then_inc(z_ready, 1)


def kernel(x, txt, L0_tok_W0, L0_tok_b0, L0_tok_W1, L0_tok_b1, L0_tok_W2, L0_tok_b2, L0_tok_Wf, L0_tok_bf,
           L0_tok_idx0, L0_tok_idx1, L0_tok_idx2, L0_attn_w_qkv, L0_attn_b_qkv, L0_attn_w_out, L0_attn_b_out,
           L0_ffn_w_router, L0_ffn_gamma1, L0_ffn_beta1, L0_ffn_w1, L0_ffn_b1, L0_ffn_w2, L0_ffn_b2):
    import concourse.bacc as bacc
    from concourse.bass_utils import run_bass_kernel_spmd

    a = {k: np.asarray(v) for k, v in locals().items() if k not in ("bacc", "run_bass_kernel_spmd")}
    x = a["x"]

    def patches(p):
        h = IMG // p
        t = x.reshape(B, CH, h, p, h, p).transpose(2, 4, 0, 3, 5, 1)
        return t.reshape(h * h, B * p * p * CH)

    def index(name, shape, order):
        i = a[name].view(np.uint32)
        return i.reshape(shape).transpose(order)

    wide, small = constants()
    bias = lambda w, b: np.concatenate([w, b[None, :]], axis=0)
    arrays = {
        "rows0": patches(1), "rows1": patches(2), "rows2": patches(4),
        "idx0": index("L0_tok_idx0", (2, P, GP), (1, 0, 2)).reshape(P, 32),
        "idx1": index("L0_tok_idx1", (64, 2, 8), (1, 0, 2)).reshape(P, 8),
        "idx2": index("L0_tok_idx2", (16, 8, 2), (1, 0, 2)).reshape(P, 2),
        "w0": a["L0_tok_W0"].T,
        "w1": a["L0_tok_W1"].T.reshape(2, 96, EMBED).transpose(1, 0, 2),
        "w2": a["L0_tok_W2"].T.reshape(8, 96, EMBED).transpose(1, 0, 2),
        "tok_bias": np.stack([a["L0_tok_b0"], a["L0_tok_b1"], a["L0_tok_b2"]], axis=1),
        "wf": a["L0_tok_Wf"].T.reshape(3, EMBED, D).transpose(1, 0, 2),
        "bf": a["L0_tok_bf"][None, :],
        "txt": a["txt"],
        "wqkv": bias(a["L0_attn_w_qkv"], a["L0_attn_b_qkv"]),
        "wout": bias(a["L0_attn_w_out"], a["L0_attn_b_out"]),
        "wr": a["L0_ffn_w_router"].T,
        "gb": np.stack([a["L0_ffn_gamma1"], a["L0_ffn_beta1"]], axis=1),
        "fc1": bias(a["L0_ffn_w1"].T, a["L0_ffn_b1"]),
        "fc2": bias(a["L0_ffn_w2"].T, a["L0_ffn_b2"]),
        "wide": wide, "small": small,
    }
    arrays = {k: np.ascontiguousarray(v) for k, v in arrays.items()}
    nc = bacc.Bacc("TRN2", target_bir_lowering=False, num_devices=1)
    args = [nc.dram_tensor(k, v.shape, mybir.dt.from_np(v.dtype), kind="ExternalInput").ap() for k, v in arrays.items()]
    out = nc.dram_tensor("out", (B, SEQ, D), F32, kind="ExternalOutput").ap()
    early_fusion(nc, *args, out)
    r = run_bass_kernel_spmd(nc, [arrays], core_ids=[0])
    return r.results[0]["out"]
```

```python
from contextlib import ExitStack

import numpy as np

import concourse.bass as bass
from concourse import mybir

F32 = mybir.dt.float32
F32R = mybir.dt.float32r
BF16 = mybir.dt.bfloat16
U32 = mybir.dt.uint32
ALU = mybir.AluOpType
ACT = mybir.ActivationFunctionType
AX_X = mybir.AxisListType.X

P = 128
B = 2
IMG = 64
CH = 3
GP = 16
EMBED = 64
D = 192
D2 = D - P
IMG_TOK = 256
TXT_TOK = 128
SEQ = IMG_TOK + TXT_TOK
TOK = B * SEQ
NT = TOK // P
TB = SEQ // P
H = 12
HD = D // H
SLOT = 64
PAIRS = H // 2
HEADS = B * H
GROUP = 3
GROUPS = HEADS // GROUP
POOL_LOW = (0, 1)
LAG = 2
AHEAD = 6
GW = GROUP * HD
VN = GW + GROUP
VW = 2 * GW + GROUP
MLP = 4 * D
MT = MLP // P
E = 4
CAP = SEQ // 2
BLOCKS = [0, 24, 48, 96, 192]
KC = MT + 2
MERGE = 512 + E * P + B * (D + 1)


def constants():
    def interp(n_in):
        pos = np.clip((np.arange(IMG_TOK) + 0.5) * (n_in / IMG_TOK) - 0.5, 0, n_in - 1)
        i0 = np.floor(pos).astype(int)
        i1 = np.minimum(i0 + 1, n_in - 1)
        w = pos - i0
        a = np.zeros((B, n_in, B, IMG_TOK), np.float32)
        for b in range(B):
            a[b, i0, b, np.arange(IMG_TOK)] += (1.0 - w).astype(np.float32)
            a[b, i1, b, np.arange(IMG_TOK)] += w.astype(np.float32)
        return a.reshape(B * n_in, B * IMG_TOK)

    wide = np.zeros((P, P + 512 + 16), np.float32)
    wide[:, :P] = np.eye(P)
    wide[:, P:P + 512] = interp(64)
    wide[:, P + 512 + 7] = 1.0
    small = np.zeros((P, MERGE + VN), np.float32)
    small[:32, :512] = interp(16)
    small[:VN, MERGE:] = np.eye(VN)
    small[VN:VW, MERGE:MERGE + GW] = np.eye(GW)
    for e in range(E):
        small[[e, E + e, 2 * E + e], 512 + e * P:512 + (e + 1) * P] = 1.0
    for b in range(B):
        at = 512 + E * P + b * (D + 1)
        for e in range(E):
            small[b * E + e, at:at + BLOCKS[e + 1]] = 1.0
            small[b * E + e, at + D] = 1.0
    return wide, small


def ring_uses():
    uses = []
    for step in range(-AHEAD, HEADS + LAG + 1):
        head = step + AHEAD
        if head < HEADS:
            uses += [("S", head, qt) for qt in range(TB)]
        if 0 < head <= HEADS and head % GROUP == 0:
            uses.append(("M", head // GROUP - 1))
        if step > GROUP + LAG - 1 and (step - LAG) % GROUP == 0:
            uses.append(("O", (step - LAG) // GROUP - 1))
    return uses


def early_fusion(nc, rows0, rows1, rows2, idx0, idx1, idx2, w0, w1, w2, tok_bias, wf, bf, txt,
                 wqkv, wout, wr, gb, fc1, fc2, wide, small, out):
    uses = ring_uses()
    use_at = {u: n for n, u in enumerate(uses)}
    with ExitStack() as ctx:
        def sb(name, shape, dt=F32):
            return ctx.enter_context(nc.sbuf_tensor(name, shape, dt))

        def sem(name):
            return ctx.enter_context(nc.semaphore(name))

        psum = ctx.enter_context(nc.psum_tensor("psum", [P, 8, 512], F32))

        wide_sb = sb("wide_sb", [P, P + 512 + 16])
        small_sb = sb("small_sb", [P, MERGE + VN])
        eye = wide_sb[:, 0:P]
        interp1 = wide_sb[:, P:P + 512]
        interp2 = small_sb[0:32, 0:512]
        eye_bf = sb("eye_bf", [P, P], BF16)
        pick_col = sb("pick_col", [P, 15], BF16)
        spread = sb("spread", [3 * E, E, P], BF16)
        masks = small_sb[0:B * E, 512 + E * P:MERGE].rearrange("p (b d) -> p b d", b=B)
        ix0 = sb("ix0", [P, 32], U32)
        ix1 = sb("ix1", [P, 8], U32)
        ix2 = sb("ix2", [P, 2], U32)
        w0_sb = sb("w0_sb", [48, EMBED])
        w1_sb = sb("w1_sb", [96, 2, EMBED])
        w2_sb = sb("w2_sb", [96, 8, EMBED])
        tok_bias_sb = sb("tok_bias_sb", [EMBED, 3])
        wf_sb = sb("wf_sb", [EMBED, 3, D])
        bf_sb = sb("bf_sb", [P, D])
        wqkv_a = sb("wqkv_a", [P, 3 * D])
        wqkv_b = sb("wqkv_b", [D2 + 1, 3 * D])
        wout_a = sb("wout_a", [P, D])
        wout_b = sb("wout_b", [D2 + 1, D])
        wr_a = sb("wr_a", [P, E])
        wr_b = sb("wr_b", [D2, E])
        gb_a = sb("gb_a", [P, 2])
        gb_b = sb("gb_b", [D2, 2])
        fc1_a = sb("fc1_a", [P, MLP])
        fc1_b = sb("fc1_b", [D2 + 1, MLP])
        fc2_sb = sb("fc2_sb", [P, KC, D])

        gelu = sb("gelu", [P, MT, TOK])
        gat0 = sb("gat0", [P, 32, 6])
        gat1 = sb("gat1", [P, 8, 24])
        gat2 = sb("gat2", [P, 2, 96])
        turned0 = sb("turned0", [48, 512])
        own0 = sb("own0", [P, 2, B, GP, CH])
        own1 = sb("own1", [P, B, 8, 12])
        own2 = sb("own2", [P, B, 2, 48])
        turned1 = sb("turned1", [96, 2, B, 64])
        turned2 = sb("turned2", [96, 8, B, 16])
        level1 = sb("level1", [P, EMBED])
        level2 = sb("level2", [32, EMBED])
        levels = gelu[0:EMBED, 0:2, :].rearrange("p c n -> p (c n)").rearrange("p (l n) -> p l n", l=3)
        fc2_b = gelu[:, 4:MT, :].rearrange("p c n -> p (c n)").rearrange("p (c d) -> p c d", c=KC)

        hid = sb("hid", [P, NT, D])
        xn = sb("xn", [P, NT, D])
        stats = sb("stats", [P, NT, 6])
        mv = sb("mv", [P, NT, 2])
        var_eps = sb("var_eps", [P, NT])
        rstd = sb("rstd", [P, NT])
        half = sb("half", [P, NT])
        x_a = sb("x_a", [P, TOK])
        x_b = sb("x_b", [D2 + 1, TOK])
        nat_q = sb("nat_q", [P, 2, H, SLOT])
        nat_k = sb("nat_k", [P, 2, H, SLOT])
        q_t = sb("q_t", [P, PAIRS, TOK], F32R)
        k_t = sb("k_t", [P, PAIRS, TOK], F32R)
        v_sb = sb("v_sb", [P, NT, H, VW + 1], F32R)
        merge = small_sb[0:VW, MERGE:MERGE + VN]
        neg_max = sb("neg_max", [P, 3, TB, GROUP])
        max_row = sb("max_row", [GROUP, 2, SEQ], F32R)
        prob = sb("prob", [P, 2, TB, SEQ])
        prob_high = sb("prob_high", [P, 3, TB, SEQ], F32R)
        prob_low = sb("prob_low", [P, 3, TB, SEQ], F32R)
        out_t = sb("out_t", [VW, 2, SEQ])
        den = sb("den", [P, 2, TB, GROUP])
        att = sb("att", [P, NT, D])
        att_a = sb("att_a", [P, TOK])
        att_b = sb("att_b", [D2 + 1, TOK])

        y0 = att
        xf_a, xf_b = att_a, att_b
        top = sb("top", [P, NT])
        gate = sb("gate", [P, NT, E])
        gsum = sb("gsum", [P, NT])
        part = sb("part", [P, NT, 3, E], BF16)
        rest = sb("rest", [P, NT, 2, E])
        gate_rows = sb("gate_rows", [3 * E, NT, P], BF16)
        ones_row = prob[0:B * E, 1, 2, :]
        beats = prob[:, 0, 0:2, :].bitcast(BF16).rearrange("p a (b n) -> p (a b) n", n=SEQ)
        rank = prob[0:B * E, 0, 0, :]
        inside = prob[0:B * E, 0, 1, :]
        last_rank = sb("last_rank", [B * E, 1])
        room = sb("room", [B * E, 1])
        at_edge = prob[0:B * E, 0, 2, :]
        place = prob[0:B * E, 1, 0, :]
        chosen = prob[0:B * E, 1, 1, :]
        weight = sb("weight", [P, NT, E])
        weight_d = xn
        acc = hid
        mlp = y0
        gate_all = gelu[:, 0:E, :].rearrange("p c (b n) -> p b c n", b=B)
        z = y0

        in_idx = sem("in_idx")
        in_tok = sem("in_tok")
        in_txt = sem("in_txt")
        in_qkv = sem("in_qkv")
        in_out = sem("in_out")
        in_fc1 = sem("in_fc1")
        in_fc2 = sem("in_fc2")
        got1 = sem("got1")
        got2 = sem("got2")
        got0 = sem("got0")
        consts_ready = sem("consts_ready")
        v_zeroed = sem("v_zeroed")
        apart = sem("apart")
        pe_tok = sem("pe_tok")
        ev_tok = sem("ev_tok")
        ev_level = sem("ev_level")
        dve_done = sem("dve_done")
        act_done = sem("act_done")
        mv_ready = sem("mv_ready")
        rstd_ready = sem("rstd_ready")
        xn_ready = sem("xn_ready")
        pe_turn = sem("pe_turn")
        turned = sem("turned")
        qkv_done = sem("qkv_done")
        high_ready = sem("high_ready")
        low_ready = sem("low_ready")
        stack_psum = sem("stack_psum")
        stack_ready = sem("stack_ready")
        stack_ready_v = sem("stack_ready_v")
        s1_done = sem("s1_done")
        max_ready = sem("max_ready")
        rows_psum = sem("rows_psum")
        rows_ready = sem("rows_ready")
        rows_in = [[sem(f"rows_in_{n}_{layer}") for n in range(GROUPS)] for layer in range(2)]
        s2_done = sem("s2_done")
        exp_ready = sem("exp_ready")
        high_probs = sem("high_probs")
        low_probs_v = sem("low_probs_v")
        low_probs_p = sem("low_probs_p")
        av_done = sem("av_done")
        out_t_ready = sem("out_t_ready")
        out_done = sem("out_done")
        norm_ready = sem("norm_ready")
        proj_done = sem("proj_done")
        hid_ready = sem("hid_ready")
        logits_done = sem("logits_done")
        logits_in = sem("logits_in")
        exp4_ready = sem("exp4_ready")
        parts_ready = sem("parts_ready")
        parts_psum = sem("parts_psum")
        gate_rows_ready = sem("gate_rows_ready")
        spread_done = sem("spread_done")
        gate_all_ready = sem("gate_all_ready")
        beats_ready = sem("beats_ready")
        rank_done = sem("rank_done")
        counted = sem("counted")
        chosen_ready = sem("chosen_ready")
        chosen_psum = sem("chosen_psum")
        coef_psum = sem("coef_psum")
        hin_ready = sem("hin_ready")
        fc1_done = sem("fc1_done")
        gelu_ready = sem("gelu_ready")
        weight_ready = sem("weight_ready")
        mlp_done = sem("mlp_done")
        mlp_copied = sem("mlp_copied")
        mlp_weighted = sem("mlp_weighted")
        mlp_added = sem("mlp_added")
        fc2_done = sem("fc2_done")
        z_ready = sem("z_ready")
        stored = sem("stored")

        block = ctx.enter_context(nc.Block())

        def s1_count(layer, head, qt):
            return layer * HEADS * TB + head * TB + qt + 1

        @block.sync
        def _(sp):
            sp.dma_start(ix1[:], idx1).then_inc(in_idx, 16)
            sp.dma_start(ix2[:], idx2).then_inc(in_idx, 16)
            sp.dma_start(ix0[:], idx0).then_inc(in_idx, 16)
            for dst, src in ((wide_sb, wide), (small_sb, small), (w1_sb, w1), (w2_sb, w2), (w0_sb, w0),
                             (tok_bias_sb, tok_bias), (wf_sb, wf)):
                sp.dma_start(dst[:], src).then_inc(in_tok, 16)
            sp.dma_start(bf_sb[:], bf[0:1, :].to_broadcast([P, D])).then_inc(in_tok, 16)
            for b in range(B):
                sp.dma_start(hid[:, TB * b + TB - 1, :], txt[b]).then_inc(in_txt, 16)
            sp.dma_start(wqkv_a[:], wqkv[0:P]).then_inc(in_qkv, 16)
            sp.dma_start(wqkv_b[:], wqkv[P:]).then_inc(in_qkv, 16)
            sp.dma_start(wout_a[:], wout[0:P]).then_inc(in_out, 16)
            sp.dma_start(wout_b[:], wout[P:]).then_inc(in_out, 16)
            sp.dma_start(wr_a[:], wr[0:P]).then_inc(in_out, 16)
            sp.dma_start(wr_b[:], wr[P:]).then_inc(in_out, 16)
            sp.dma_start(gb_a[:], gb[0:P]).then_inc(in_out, 16)
            sp.dma_start(gb_b[:], gb[P:]).then_inc(in_out, 16)
            sp.dma_start(fc1_a[:], fc1[0:P, 0:MLP]).then_inc(in_fc1, 16)
            sp.dma_start(fc1_b[:], fc1[P:, 0:MLP]).then_inc(in_fc1, 16)
            for half, dst in enumerate((fc2_sb, fc2_b)):
                cols = slice(half * D, (half + 1) * D)
                sp.dma_start(dst[:, 0:KC - 1, :], fc2[0:(KC - 1) * P, cols].rearrange("(c p) d -> p c d", p=P)).then_inc(in_fc2, 16)
                sp.dma_start(dst[0:D2 + 1, KC - 1, :], fc2[(KC - 1) * P:, cols]).then_inc(in_fc2, 16)

            sp.wait_ge(qkv_done, NT)
            sp.dma_start(wqkv_a[:], fc1[0:P, MLP:]).then_inc(in_qkv, 16)
            sp.dma_start(wqkv_b[:], fc1[P:, MLP:]).then_inc(in_qkv, 16)

            for layer in range(2):
                for g in range(GROUPS):
                    sp.wait_ge(rows_ready, layer * GROUPS + g + 1)
                    for n in range(GROUP):
                        b, h = divmod(g * GROUP + n, H)
                        at = SLOT * (h % 2) + 3 * HD
                        sp.dma_start(q_t[at:at + 1, h // 2, b * SEQ:(b + 1) * SEQ].bitcast(F32),
                                     max_row[n:n + 1, g % 2, :].bitcast(F32)).then_inc(rows_in[layer][g], 16)
            for t in range(NT):
                b, p = divmod(t, TB)
                sp.wait_ge(z_ready, t + 1)
                sp.dma_start(out[b, p * P:(p + 1) * P, :], z[:, t, :]).then_inc(stored, 16)
            sp.wait_ge(stored, 16 * NT)

        def low_probs(engine, layer, head, kt, done):
            engine.wait_ge(high_probs, layer * HEADS + head + 1)
            if layer * HEADS + head >= 3:
                engine.wait_ge(av_done, layer * HEADS + head - 2)
            engine.tensor_tensor(prob_low[:, head % 3, kt, :], prob[:, head % 2, kt, :],
                                 prob_high[:, head % 3, kt, :].bitcast(F32), ALU.subtract).then_inc(done, 1)

        @block.gpsimd
        def _(pool):
            pool.wait_ge(in_idx, 48)

            def gather(dst, rows, index, done):
                nc.gpsimd.indirect_dma_start(
                    out=dst, out_offset=None, in_=rows,
                    in_offset=bass.IndirectOffsetOnAxis(ap=index, axis=0)).then_inc(done, 16)

            for j in range(8):
                gather(gat1[:, j, :], rows1, ix1[:, j:j + 1], got1)
            for j in range(2):
                gather(gat2[:, j, :], rows2, ix2[:, j:j + 1], got2)
            for j in range(32):
                gather(gat0[:, j, :], rows0, ix0[:, j:j + 1], got0)

            pool.wait_ge(consts_ready, 1)
            def root(n):
                pool.wait_ge(mv_ready, n + 1)
                pool.tensor_tensor(rstd[:], var_eps[:], half[:], ALU.pow).then_inc(rstd_ready, 1)

            for layer in range(2):
                for n in range(layer, 2 * layer + 1):
                    root(n)
                if layer == 1:
                    pool.wait_ge(weight_ready, 1)
                    for t in range(NT):
                        pool.wait_ge(mlp_copied, t + 1)
                        pool.tensor_tensor(mlp[:, t, :], mlp[:, t, :], weight_d[:, t, :], ALU.mult).then_inc(mlp_weighted, 1)
                        pool.wait_ge(mlp_weighted, t + 1)
                        pool.tensor_tensor(acc[:, t, :], acc[:, t, :], mlp[:, t, :], ALU.add).then_inc(mlp_added, 1)
                for head in range(HEADS):
                    for kt in POOL_LOW:
                        low_probs(pool, layer, head, kt, low_probs_p)

        @block.tensor
        def _(pe):
            mm = nc.tensor.matmul

            pe.wait_ge(in_tok, 128)
            pe.wait_ge(apart, 1)
            for b in range(B):
                last = nc.tensor.transpose(psum[0:96, 0, b * P:(b + 1) * P], own1[:, b].rearrange("p j c -> p (j c)"), eye)
            last.then_inc(pe_tok, 1)
            pe.wait_ge(apart, 2)
            for b in range(B):
                last = nc.tensor.transpose(psum[0:96, 1, b * P:(b + 1) * P], own2[:, b].rearrange("p j c -> p (j c)"), eye)
            last.then_inc(pe_tok, 1)
            pe.wait_ge(ev_tok, 1)
            for jh in range(2):
                last = mm(psum[:, 2, 0:EMBED], turned1[:, jh].rearrange("p b g -> p (b g)"), w1_sb[:, jh, :],
                          start=jh == 0, stop=jh == 1)
            last.then_inc(pe_tok, 1)
            pe.wait_ge(ev_tok, 2)
            for jh in range(8):
                last = mm(psum[0:32, 3, 0:EMBED], turned2[:, jh].rearrange("p b g -> p (b g)"), w2_sb[:, jh, :],
                          start=jh == 0, stop=jh == 7)
            last.then_inc(pe_tok, 1)
            pe.wait_ge(ev_tok, 3)
            mm(psum[0:EMBED, 4, :], level1[:], interp1, start=True, stop=True).then_inc(pe_tok, 1)
            pe.wait_ge(ev_tok, 4)
            mm(psum[0:EMBED, 5, :], level2[:], interp2, start=True, stop=True).then_inc(pe_tok, 1)
            pe.wait_ge(apart, 3)
            for n in range(4):
                b, gt = divmod(n, 2)
                last = nc.tensor.transpose(psum[0:48, 6, n * P:(n + 1) * P],
                                           own0[:, gt, b].rearrange("p j c -> p (j c)"), eye)
            last.then_inc(pe_tok, 1)
            pe.wait_ge(ev_level, 3)
            mm(psum[0:EMBED, 7, :], w0_sb[:], turned0[:], start=True, stop=True).then_inc(pe_tok, 1)
            pe.wait_ge(ev_level, 4)
            for n in range(4):
                for lv in range(3):
                    last = mm(psum[:, n, 0:D], levels[:, lv, n * P:(n + 1) * P], wf_sb[:, lv, :],
                              start=lv == 0, stop=lv == 2)
                last.then_inc(pe_tok, 1)

            def turn(src, t, bank, done):
                nc.tensor.transpose(psum[:, bank, 0:P], src[:, t, 0:P], eye)
                nc.tensor.transpose(psum[0:D2, bank, P:2 * P], src[:, t, P:D], eye).then_inc(done, 1)

            def project(layer, weights, at):
                wa, wb = weights

                def stack_copied(n, u):
                    if u == 1:
                        pe.wait_ge(stack_ready_v, n + 1)
                    else:
                        pe.wait_ge(stack_ready, 2 * n + (u > 0) + 1)

                def stacks(t):
                    pe.wait_ge(high_ready, 2 * (layer * NT + t + 1))
                    pe.wait_ge(low_ready, layer * NT + t + 1)
                    for u in range(3):
                        if layer * NT + t >= 1:
                            stack_copied(layer * NT + t - 1, u)
                        for i in range(4):
                            c = 4 * u + i
                            nat = (nat_q, nat_k)[c // PAIRS]
                            pair = c % PAIRS
                            last = nc.tensor.transpose(
                                psum[:, 5 + u, i * P:(i + 1) * P],
                                nat[:, t % 2, 2 * pair:2 * pair + 2, :], eye)
                        last.then_inc(stack_psum, 1)

                def turn_input(t):
                    pe.wait_ge(xn_ready, t + 1)
                    if t >= 1:
                        pe.wait_ge(turned, t)
                    turn(xn, t, 4, pe_turn)

                if layer == 0:
                    turn_input(0)
                for t in range(NT):
                    if layer == 0:
                        if t + 1 < NT:
                            turn_input(t + 1)
                        pe.wait_ge(turned, t + 1)
                    else:
                        pe.wait_ge(hin_ready, t // TB + 1)
                    if t >= 2:
                        pe.wait_ge(high_ready, 2 * (layer * NT + t - 1))
                        pe.wait_ge(low_ready, layer * NT + t - 1)
                    tok = slice(t * P, (t + 1) * P)
                    for bank, w in ((2 * (t % 2), slice(at, at + 2 * D)),
                                    (2 * (t % 2) + 1, slice(at + 2 * D, at + 3 * D))):
                        n = w.stop - w.start
                        mm(psum[:, bank, 0:n], x_a[:, tok], wa[:, w], start=True, stop=False)
                        last = mm(psum[:, bank, 0:n], x_b[:, tok], wb[:, w], start=False, stop=True)
                    last.then_inc(qkv_done, 1)
                    if t >= 1:
                        stacks(t - 1)
                stacks(NT - 1)

            def keep_clock():
                mm(psum[:, 7, 0:256], eye, wide_sb[:, 0:256], start=True, stop=True)

            def feed_forward_down(t, third):
                pe.wait_ge(gelu_ready, B * MT)
                if t >= 2:
                    pe.wait_ge(mlp_copied, t - 1)
                for c in range(third * MT // TB, (third + 1) * MT // TB):
                    last = mm(psum[:, 6 + t % 2, 0:D], gelu[:, c, t * P:(t + 1) * P], fc2_sb[:, c, :],
                              start=c == 0, stop=c == MT - 1)
                if third == TB - 1:
                    last.then_inc(mlp_done, 1)

            def attention(layer):
                def free_ring_bank(n):
                    if n < 2:
                        return
                    if uses[n - 2][0] == "S":
                        pe.wait_ge(max_ready, s1_count(layer, uses[n - 2][1], uses[n - 2][2]))
                    elif uses[n - 2][0] == "O":
                        pe.wait_ge(norm_ready, layer * GROUPS + uses[n - 2][1] + 1)
                    else:
                        pe.wait_ge(rows_ready, layer * GROUPS + uses[n - 2][1] + 1)

                def scores_for_max(head, qt):
                    b, h = divmod(head, H)
                    rows = slice(SLOT * (h % 2), SLOT * (h % 2) + 3 * HD)
                    n = use_at[("S", head, qt)]
                    free_ring_bank(n)
                    mm(psum[:, n % 2, 0:SEQ], q_t[rows, h // 2, b * SEQ + qt * P:b * SEQ + (qt + 1) * P],
                       k_t[rows, h // 2, b * SEQ:(b + 1) * SEQ], start=True, stop=True).then_inc(s1_done, 1)

                def turn_maxima(g):
                    n = use_at[("M", g)]
                    free_ring_bank(n)
                    pe.wait_ge(max_ready, s1_count(layer, g * GROUP + GROUP - 1, TB - 1))
                    for qt in range(TB):
                        last = nc.tensor.transpose(psum[0:GROUP, n % 2, qt * P:(qt + 1) * P],
                                                   neg_max[:, g % 3, qt, :], eye)
                    last.then_inc(rows_psum, 1)

                def scores_for_exp(head):
                    b, h = divmod(head, H)
                    rows = slice(SLOT * (h % 2), SLOT * (h % 2) + 3 * HD + 1)
                    if head % GROUP == 0:
                        pe.wait_ge(rows_in[layer][head // GROUP], 16 * GROUP)
                    for kt in range(TB):
                        n = layer * HEADS * TB + head * TB + kt
                        if n >= 4:
                            pe.wait_ge(exp_ready, n - 3)
                        mm(psum[:, 2 + n % 4, 0:SEQ], k_t[rows, h // 2, b * SEQ + kt * P:b * SEQ + (kt + 1) * P],
                           q_t[rows, h // 2, b * SEQ:(b + 1) * SEQ], start=True, stop=True).then_inc(s2_done, 1)

                def weigh_values(head, kt):
                    b, h = divmod(head, H)
                    g, hl = divmod(head, GROUP)
                    if hl == 0 and kt == 0 and g >= 2:
                        pe.wait_ge(out_t_ready, layer * GROUPS + g - 1)
                    elif hl == 0 and kt == 0 and layer == 1:
                        pe.wait_ge(mlp_copied, NT)
                    pe.wait_ge(high_probs, layer * HEADS + head + 1)
                    mm(psum[0:VW, 6 + g % 2, 0:SEQ], v_sb[:, TB * b + kt, h, 0:VW], prob_high[:, head % 3, kt, :],
                       start=hl == 0 and kt == 0, stop=False)
                    if kt in POOL_LOW:
                        pe.wait_ge(low_probs_p, len(POOL_LOW) * (layer * HEADS + head) + POOL_LOW.index(kt) + 1)
                    else:
                        pe.wait_ge(low_probs_v, layer * HEADS + head + 1)
                    last = mm(psum[0:VW, 6 + g % 2, 0:SEQ], v_sb[:, TB * b + kt, h, 0:VW], prob_low[:, head % 3, kt, :],
                              start=False, stop=hl == GROUP - 1 and kt == TB - 1)
                    if kt == TB - 1:
                        last.then_inc(av_done, 1)

                def turn_output(g):
                    n = use_at[("O", g)]
                    free_ring_bank(n)
                    pe.wait_ge(out_t_ready, layer * GROUPS + g + 1)
                    for qt in range(TB):
                        last = mm(psum[:, n % 2, qt * VN:(qt + 1) * VN], out_t[:, g % 2, qt * P:(qt + 1) * P], merge,
                                  start=True, stop=True)
                    last.then_inc(out_done, 1)

                pe.wait_ge(stack_ready, 2 * NT * (layer + 1))
                pe.wait_ge(stack_ready_v, NT * (layer + 1))
                for step in range(-AHEAD, HEADS + LAG + 1):
                    if 0 <= step < HEADS:
                        scores_for_exp(step)
                    head = step + AHEAD
                    for n in range(TB):
                        if head < HEADS:
                            scores_for_max(head, n)
                        if layer == 0 and step < LAG:
                            keep_clock()
                        if layer == 1 and LAG - NT <= step < LAG:
                            feed_forward_down(step + NT - LAG, n)
                        if LAG <= step < HEADS + LAG:
                            weigh_values(step - LAG, n)
                    if 0 < head <= HEADS and head % GROUP == 0:
                        turn_maxima(head // GROUP - 1)
                    if step > GROUP + LAG - 1 and (step - LAG) % GROUP == 0:
                        turn_output((step - LAG) // GROUP - 1)

            pe.wait_ge(in_qkv, 32)
            project(0, (wqkv_a, wqkv_b), 0)
            attention(0)

            pe.wait_ge(in_out, 96)
            for t in range(NT):
                pe.wait_ge(norm_ready, GROUPS // B * (t // TB + 1))
                if t >= 2:
                    pe.wait_ge(turned, NT + t - 1)
                turn(att, t, 4 + t % 2, pe_turn)
                pe.wait_ge(turned, NT + t + 1)
                if t >= 2:
                    pe.wait_ge(hid_ready, t - 1)
                tok = slice(t * P, (t + 1) * P)
                mm(psum[:, 2 + t % 2, 0:D], att_a[:, tok], wout_a[:], start=True, stop=False)
                mm(psum[:, 2 + t % 2, 0:D], att_b[:, tok], wout_b[:], start=False, stop=True).then_inc(proj_done, 1)

            for t in range(NT):
                pe.wait_ge(xn_ready, NT + t + 1)
                if t >= 2:
                    pe.wait_ge(turned, 2 * NT + t - 1)
                turn(xn, t, 4 + t % 2, pe_turn)
            for t in range(NT):
                pe.wait_ge(turned, 2 * NT + t + 1)
                tok = slice(t * P, (t + 1) * P)
                mm(psum[:, 6, t * E:(t + 1) * E], xf_a[:, tok], wr_a[:], start=True, stop=False)
                last = mm(psum[:, 6, t * E:(t + 1) * E], xf_b[0:D2, tok], wr_b[:], start=False, stop=True)
            last.then_inc(logits_done, 1)
            for t in range(NT):
                pe.wait_ge(xn_ready, 2 * NT + t + 1)
                if t >= 2:
                    pe.wait_ge(turned, 3 * NT + t - 1)
                turn(y0, t, 4 + t % 2, pe_turn)
            pe.wait_ge(parts_ready, 1)
            for t in range(NT):
                last = nc.tensor.transpose(
                    psum[0:3 * E, 7, t * (P // 2):(t + 1) * (P // 2)].bitcast(BF16),
                    part[:, t].rearrange("p a e -> p (a e)"), eye_bf[:])
            last.then_inc(parts_psum, 1)
            pe.wait_ge(gate_rows_ready, 1)
            for b in range(B):
                for e in range(E):
                    n = b * E + e
                    if n >= 4:
                        pe.wait_ge(gate_all_ready, n - 3)
                    mm(psum[:, n % 4, 0:SEQ], spread[:, e, :], gate_rows[:, TB * b:TB * (b + 1), :],
                       start=True, stop=True).then_inc(spread_done, 1)
            for n in range(B * E * TB):
                pe.wait_ge(beats_ready, n + 1)
                be = n // TB
                mm(psum[0:B * E, 6, 0:SEQ], pick_col[:, 7 - be:15 - be], beats[:, n % 4, :],
                   start=n == 0, stop=n == B * E * TB - 1).then_inc(counted, 1)
            pe.wait_ge(chosen_ready, 1)
            for b in range(B):
                mm(psum[:, b, 0:SEQ], masks[:, b, 0:P], chosen[:], start=True, stop=True)
                mm(psum[0:D2 + 1, 2 + b, 0:SEQ], masks[:, b, P:D + 1], chosen[:],
                   start=True, stop=True).then_inc(coef_psum, 1)
            for p in range(TB):
                last = nc.tensor.transpose(psum[:, 6, p * B * E:(p + 1) * B * E], chosen[:, p * P:(p + 1) * P],
                                           eye[0:B * E, 0:B * E])
            last.then_inc(chosen_psum, 1)

            pe.wait_ge(in_fc1, 32)
            for n in range(B * MT):
                b, f = divmod(n, MT)
                pe.wait_ge(hin_ready, b + 1)
                if n >= 2:
                    pe.wait_ge(gelu_ready, n - 1)
                tok = slice(b * SEQ, (b + 1) * SEQ)
                mm(psum[:, 4 + n % 2, 0:SEQ], fc1_a[:, f * P:(f + 1) * P], x_a[:, tok], start=True, stop=False)
                mm(psum[:, 4 + n % 2, 0:SEQ], fc1_b[:, f * P:(f + 1) * P], x_b[:, tok],
                   start=False, stop=True).then_inc(fc1_done, 1)

            pe.wait_ge(in_qkv, 64)
            project(1, (wqkv_a, wqkv_b), 0)
            attention(1)

            for t in range(NT):
                pe.wait_ge(norm_ready, GROUPS + GROUPS // B * (t // TB + 1))
                if t >= 2:
                    pe.wait_ge(turned, 4 * NT + t - 1)
                turn(att, t, 4 + t % 2, pe_turn)
                if t >= 2:
                    pe.wait_ge(z_ready, t - 1)
                tok = slice(t * P, (t + 1) * P)
                pe.wait_ge(turned, 4 * NT + t + 1)
                mm(psum[:, 2 + t % 2, 0:D], att_a[:, tok], fc2_sb[:, MT, :], start=True, stop=False)
                mm(psum[:, 2 + t % 2, 0:D], att_b[:, tok], fc2_sb[0:D2 + 1, MT + 1, :],
                   start=False, stop=True).then_inc(fc2_done, 1)

        @block.scalar
        def _(act):
            act.wait_ge(pe_tok, 5)
            act.wait_ge(in_tok, 128)
            act.activation(levels[:, 1, :], psum[0:EMBED, 4, :], ACT.Identity, bias=tok_bias_sb[:, 1:2]).then_inc(ev_level, 1)
            act.wait_ge(pe_tok, 6)
            act.activation(levels[:, 2, :], psum[0:EMBED, 5, :], ACT.Identity, bias=tok_bias_sb[:, 2:3]).then_inc(ev_level, 1)
            act.wait_ge(pe_tok, 7)
            act.activation(turned0[:], psum[0:48, 6, :], ACT.Copy).then_inc(ev_level, 1)
            act.wait_ge(pe_tok, 8)
            act.activation(levels[:, 0, :], psum[0:EMBED, 7, :], ACT.Identity, bias=tok_bias_sb[:, 0:1]).then_inc(ev_level, 1)

            def copy_turned(n, bank, dst_a, dst_b):
                t = n % NT
                tok = slice(t * P, (t + 1) * P)
                act.wait_ge(pe_turn, n + 1)
                act.activation(dst_a[:, tok], psum[:, bank, 0:P], ACT.Copy)
                act.activation(dst_b[0:D2, tok], psum[0:D2, bank, P:2 * P], ACT.Copy).then_inc(turned, 1)

            def stacks(layer, t):
                for u in (0, 2):
                    n = 3 * (layer * NT + t) + u
                    act.wait_ge(stack_psum, n + 1)
                    pair = 0 if u == 0 else 2
                    act.activation((q_t if u == 0 else k_t)[:, pair:pair + 4, t * P:(t + 1) * P],
                                   psum[:, 5 + u, :].rearrange("p (a b) -> p a b", b=P), ACT.Copy).then_inc(stack_ready, 1)

            def project(layer):
                if layer == 0:
                    copy_turned(0, 4, x_a, x_b)
                for t in range(NT):
                    if layer == 0 and t + 1 < NT:
                        copy_turned(t + 1, 4, x_a, x_b)
                    act.wait_ge(qkv_done, layer * NT + t + 1)
                    if t == 0:
                        act.wait_ge(consts_ready, 1)
                    if layer * NT + t >= 2:
                        act.wait_ge(stack_psum, 3 * (layer * NT + t - 1))
                    src = psum[:, 2 * (t % 2), 0:2 * D].rearrange("p (s h d) -> p s h d", s=2, h=H)
                    for s, nat, slots in ((0, nat_q, (0, 2)), (1, nat_k, (0, 1))):
                        dst = nat[:, t % 2].bitcast(F32R)
                        for n, slot in enumerate(slots):
                            last = act.activation(dst[:, :, slot * HD:(slot + 1) * HD], src[:, s], ACT.Copy)
                        last.then_inc(high_ready, 1)
                    if t >= 1:
                        stacks(layer, t - 1)
                stacks(layer, NT - 1)

            def attention(layer):
                for step in range(-AHEAD, HEADS + LAG + 1):
                    if 0 <= step < HEADS:
                        for kt in range(TB):
                            n = layer * HEADS * TB + step * TB + kt
                            act.wait_ge(s2_done, n + 1)
                            if layer * HEADS + step >= 2 and kt == 0:
                                act.wait_ge(low_probs_v, layer * HEADS + step - 1)
                                act.wait_ge(low_probs_p, len(POOL_LOW) * (layer * HEADS + step - 1))
                            act.activation(prob[:, step % 2, kt, :], psum[:, 2 + n % 4, 0:SEQ], ACT.Exp,
                                           scale=float(HD) ** -0.5).then_inc(exp_ready, 1)
                    if step > GROUP + LAG - 1 and (step - LAG) % GROUP == 0:
                        g = (step - LAG) // GROUP - 1
                        act.wait_ge(av_done, layer * HEADS + (g + 1) * GROUP)
                        act.activation(out_t[:, g % 2, :], psum[0:VW, 6 + g % 2, 0:SEQ], ACT.Copy).then_inc(out_t_ready, 1)
                    if 0 <= step < HEADS:
                        act.wait_ge(exp_ready, n + 1)
                        if layer * HEADS + step >= 3:
                            act.wait_ge(av_done, layer * HEADS + step - 2)
                        act.activation(prob_high[:, step % 3], prob[:, step % 2], ACT.Copy).then_inc(high_probs, 1)
                    if layer == 1 and LAG - NT <= step < LAG:
                        t = step + NT - LAG
                        act.wait_ge(mlp_done, t + 1)
                        act.activation(mlp[:, t, :], psum[:, 6 + t % 2, 0:D], ACT.Copy).then_inc(mlp_copied, 1)
                    head = step + AHEAD
                    if 0 < head <= HEADS and head % GROUP == 0:
                        g = head // GROUP - 1
                        act.wait_ge(rows_psum, layer * GROUPS + g + 1)
                        if g >= 2:
                            act.wait_ge(rows_in[layer][g - 2], 16 * GROUP)
                        elif layer:
                            act.wait_ge(rows_in[0][GROUPS - 2 + g], 16 * GROUP)
                        act.activation(max_row[:, g % 2, :], psum[0:GROUP, use_at[("M", g)] % 2, 0:SEQ],
                                       ACT.Copy).then_inc(rows_ready, 1)

            project(0)
            attention(0)
            for t in range(NT):
                copy_turned(NT + t, 4 + t % 2, att_a, att_b)
            for t in range(NT):
                copy_turned(2 * NT + t, 4 + t % 2, xf_a, xf_b)
            act.wait_ge(logits_in, 1)
            act.activation(gate[:], gate[:], ACT.Exp).then_inc(exp4_ready, 1)
            for t in range(NT):
                tok = slice(t * P, (t + 1) * P)
                act.wait_ge(pe_turn, 3 * NT + t + 1)
                act.activation(x_a[:, tok], psum[:, 4 + t % 2, 0:P], ACT.Identity, scale=gb_a[:, 0:1], bias=gb_a[:, 1:2])
                act.activation(x_b[0:D2, tok], psum[0:D2, 4 + t % 2, P:2 * P], ACT.Identity,
                               scale=gb_b[:, 0:1], bias=gb_b[:, 1:2]).then_inc(turned, 1)
            act.wait_ge(parts_psum, 1)
            act.activation(gate_rows[:], psum[0:3 * E, 7, 0:NT * P // 2].bitcast(BF16).rearrange("p (t b) -> p t b", b=P), ACT.Copy)\
               .then_inc(gate_rows_ready, 1)
            for b in range(B):
                for e in range(E):
                    n = b * E + e
                    act.wait_ge(spread_done, n + 1)
                    act.activation(gate_all[:, b, e, :], psum[:, n % 4, 0:SEQ], ACT.Copy).then_inc(gate_all_ready, 1)
            for n in range(B * MT):
                b, f = divmod(n, MT)
                act.wait_ge(fc1_done, n + 1)
                act.activation(gelu[:, f, b * SEQ:(b + 1) * SEQ], psum[:, 4 + n % 2, 0:SEQ], ACT.Gelu).then_inc(gelu_ready, 1)
            project(1)
            attention(1)
            for t in range(NT):
                copy_turned(4 * NT + t, 4 + t % 2, att_a, att_b)

        @block.vector
        def _(dve):
            chain = [0]

            def link(instruction):
                chain[0] += 1
                instruction.then_inc(dve_done, 1)
                dve.wait_ge(dve_done, chain[0])

            dve.memset(half[:], -0.5)
            dve.memset(x_b[D2:D2 + 1, :], 1.0)
            dve.memset(att_b[D2:D2 + 1, :], 1.0)
            dve.memset(v_sb[:].bitcast(F32), 0.0).then_inc(v_zeroed, 1)
            dve.wait_ge(v_zeroed, 1)
            for hl in range(GROUP):
                dve.memset(v_sb[:, :, hl:H:GROUP, GW + hl:GW + hl + 1].bitcast(F32), 1.0)
            dve.memset(nat_q[:], 0.0)
            dve.memset(nat_k[:], 1.0).then_inc(consts_ready, 1)
            dve.wait_ge(in_tok, 128)
            dve.tensor_copy(eye_bf[:], eye)
            dve.tensor_copy(pick_col[:], wide_sb[:, P + 512:P + 512 + 15])
            link(dve.tensor_copy(spread[:], small_sb[0:3 * E, 512:512 + E * P].rearrange("p (e n) -> p e n", e=E)))
            dve.wait_ge(got1, 8 * 16)
            dve.tensor_copy(own1[:], gat1[:].rearrange("p j (b c) -> p b j c", b=B)).then_inc(apart, 1)
            dve.wait_ge(got2, 2 * 16)
            dve.tensor_copy(own2[:], gat2[:].rearrange("p j (b c) -> p b j c", b=B)).then_inc(apart, 1)
            dve.wait_ge(pe_tok, 1)
            dve.tensor_copy(turned1[:], psum[0:96, 0, 0:B * P].rearrange("p (b j g) -> p j b g", b=B, j=2)).then_inc(ev_tok, 1)
            dve.wait_ge(pe_tok, 2)
            dve.tensor_copy(turned2[:], psum[0:96, 1, 0:B * P].rearrange("p (b j g) -> p j b g", b=B, j=8)).then_inc(ev_tok, 1)
            dve.wait_ge(pe_tok, 3)
            dve.tensor_copy(level1[:], psum[:, 2, 0:EMBED]).then_inc(ev_tok, 1)
            dve.wait_ge(pe_tok, 4)
            dve.tensor_copy(level2[:], psum[0:32, 3, 0:EMBED]).then_inc(ev_tok, 1)
            dve.wait_ge(in_fc2, 64)
            dve.tensor_tensor(fc2_sb[:, 0:KC - 1, :], fc2_sb[:, 0:KC - 1, :], fc2_b[:, 0:KC - 1, :], ALU.add)
            link(dve.tensor_tensor(fc2_sb[0:D2 + 1, KC - 1, :], fc2_sb[0:D2 + 1, KC - 1, :],
                                   fc2_b[0:D2 + 1, KC - 1, :], ALU.add))
            dve.wait_ge(got0, 32 * 16)
            for gt in range(2):
                last = dve.tensor_copy(own0[:, gt], gat0[:, GP * gt:GP * (gt + 1), :].rearrange("p j (b c) -> p b j c", b=B))
            last.then_inc(apart, 1)
            for n in range(4):
                b, gt = divmod(n, 2)
                dve.wait_ge(pe_tok, 9 + n)
                last = dve.tensor_tensor(hid[:, TB * b + gt, :], psum[:, n, 0:D], bf_sb[:], ALU.add)
            link(last)
            dve.wait_ge(in_txt, 32)

            def layer_norm(n, src, dst, eps, ready):
                for t in range(NT):
                    last = dve.bn_stats(stats[:, t, :], src[:, t, :])
                link(last)
                for t in range(NT):
                    last = dve.bn_aggr(mv[:, t, :], stats[:, t, :])
                link(last)
                dve.tensor_scalar(var_eps[:], mv[:, :, 1], eps, None, ALU.add).then_inc(mv_ready, 1)
                dve.wait_ge(rstd_ready, n + 1)
                for t in range(NT):
                    dve.tensor_scalar(dst[:, t, :], src[:, t, :], mv[:, t, 0:1], rstd[:, t:t + 1],
                                      ALU.subtract, ALU.mult).then_inc(ready, 1)

            def middle_stack(layer, t):
                n = 3 * (layer * NT + t) + 1
                dve.wait_ge(stack_psum, n + 1)
                for dst, pair, i in ((q_t, 4, 0), (k_t, 0, 2)):
                    last = dve.tensor_copy(dst[:, pair:pair + 2, t * P:(t + 1) * P],
                                           psum[:, 6, i * P:(i + 2) * P].rearrange("p (a b) -> p a b", b=P))
                last.then_inc(stack_ready_v, 1)

            def project(layer):
                for t in range(NT):
                    dve.wait_ge(high_ready, 2 * (layer * NT + t + 1))
                    bank = psum[:, 2 * (t % 2), 0:2 * D].rearrange("p (s h d) -> p s h d", s=2, h=H)
                    dve.tensor_tensor(nat_q[:, t % 2, :, HD:2 * HD].bitcast(F32R), bank[:, 0], nat_q[:, t % 2, :, 0:HD], ALU.subtract)
                    dve.tensor_tensor(nat_k[:, t % 2, :, 2 * HD:3 * HD].bitcast(F32R), bank[:, 1], nat_k[:, t % 2, :, 0:HD], ALU.subtract)
                    v = psum[:, 2 * (t % 2) + 1, 0:D].rearrange("p (g h d) -> p g h d", h=GROUP, d=HD)
                    dst = v_sb[:, t].rearrange("p (g h) w -> p g h w", h=GROUP)
                    for hl in range(GROUP):
                        high = dst[:, :, hl, hl * HD:(hl + 1) * HD]
                        last = dve.tensor_copy(high, v[:, :, hl, :])
                    link(last)
                    for hl in range(GROUP):
                        high = dst[:, :, hl, hl * HD:(hl + 1) * HD]
                        last = dve.tensor_tensor(dst[:, :, hl, VN + hl * HD:VN + (hl + 1) * HD], v[:, :, hl, :],
                                                 high.bitcast(F32), ALU.subtract)
                    last.then_inc(low_ready, 1)
                    if t >= 1:
                        middle_stack(layer, t - 1)
                middle_stack(layer, NT - 1)

            def attention(layer):
                def normalise(g):
                    b, h0 = divmod(g * GROUP, H)
                    dve.wait_ge(out_done, layer * GROUPS + g + 1)
                    if layer == 1 and g == 0:
                        dve.wait_ge(mlp_added, NT)
                    o = psum[:, use_at[("O", g)] % 2, 0:TB * VN].rearrange("p (q n) -> p q n", q=TB)
                    link(dve.reciprocal(den[:, g % 2], o[:, :, GW:VN]))
                    dst = att[:, TB * b:TB * (b + 1), h0 * HD:(h0 + GROUP) * HD].rearrange("p q (h d) -> p q h d", h=GROUP)
                    dve.tensor_tensor(dst, o[:, :, 0:GW].rearrange("p q (h d) -> p q h d", h=GROUP),
                                      den[:, g % 2].rearrange("p q (h o) -> p q h o", o=1).to_broadcast([P, TB, GROUP, HD]),
                                      ALU.mult).then_inc(norm_ready, 1)

                for step in range(-AHEAD, HEADS + LAG + 1):
                    head = step + AHEAD
                    if head < HEADS:
                        g, hl = divmod(head, GROUP)
                        for qt in range(TB):
                            if qt == 1 and 1 <= step <= HEADS:
                                low_probs(dve, layer, step - 1, TB - 1, low_probs_v)
                            dve.wait_ge(s1_done, s1_count(layer, head, qt))
                            if hl == 0 and qt == 0 and g >= 3:
                                dve.wait_ge(rows_psum, layer * GROUPS + g - 2)
                            dve.tensor_reduce(neg_max[:, g % 3, qt, hl:hl + 1], psum[:, use_at[("S", head, qt)] % 2, 0:SEQ],
                                              AX_X, ALU.max, negate=True).then_inc(max_ready, 1)
                    elif 1 <= step <= HEADS:
                        low_probs(dve, layer, step - 1, TB - 1, low_probs_v)
                    if step > GROUP + LAG - 1 and (step - LAG) % GROUP == 0:
                        normalise((step - LAG) // GROUP - 1)

            layer_norm(0, hid, xn, 1e-5, xn_ready)
            project(0)
            attention(0)

            for t in range(NT):
                dve.wait_ge(proj_done, t + 1)
                last = dve.tensor_tensor(hid[:, t, :], psum[:, 2 + t % 2, 0:D], hid[:, t, :], ALU.add)
                if t < NT - 1:
                    last.then_inc(hid_ready, 1)
            link(last)
            layer_norm(1, hid, xn, 1e-5, xn_ready)
            dve.wait_ge(xn_ready, 2 * NT)
            link(dve.tensor_tensor(acc[:], hid[:], xn[:], ALU.add))
            layer_norm(2, xn, y0, 1e-6, xn_ready)

            dve.wait_ge(logits_done, 1)
            logits = psum[:, 6, 0:NT * E].rearrange("p (t e) -> p t e", e=E)
            link(dve.tensor_reduce(top[:], logits, AX_X, ALU.max))
            dve.tensor_tensor(gate[:], logits, top[:].rearrange("p (t o) -> p t o", o=1).to_broadcast([P, NT, E]),
                              ALU.subtract).then_inc(logits_in, 1)
            dve.wait_ge(exp4_ready, 1)
            link(dve.tensor_reduce(gsum[:], gate[:], AX_X, ALU.add))
            link(dve.reciprocal(gsum[:], gsum[:]))
            link(dve.tensor_tensor(gate[:], gate[:], gsum[:].rearrange("p (t o) -> p t o", o=1).to_broadcast([P, NT, E]), ALU.mult))
            link(dve.tensor_copy(part[:, :, 0, :], gate[:]))
            link(dve.tensor_tensor(rest[:, :, 0, :], gate[:], part[:, :, 0, :], ALU.subtract))
            link(dve.tensor_copy(part[:, :, 1, :], rest[:, :, 0, :]))
            link(dve.tensor_tensor(rest[:, :, 1, :], rest[:, :, 0, :], part[:, :, 1, :], ALU.subtract))
            dve.tensor_copy(part[:, :, 2, :], rest[:, :, 1, :]).then_inc(parts_ready, 1)

            for n in range(B * E * TB):
                be, mt = divmod(n, TB)
                b, e = divmod(be, E)
                dve.wait_ge(gate_all_ready, be + 1)
                if n >= 4:
                    dve.wait_ge(counted, n - 3)
                dve.tensor_scalar(beats[:, n % 4, :], gate_all[:, b, e, :], gate[:, TB * b + mt, e:e + 1], None,
                                  ALU.is_lt).then_inc(beats_ready, 1)
            dve.wait_ge(counted, B * E * TB)
            dve.memset(ones_row[:], 1.0)
            link(dve.tensor_copy(rank[:], psum[0:B * E, 6, 0:SEQ]))
            link(dve.tensor_scalar(inside[:], rank[:], float(CAP), None, ALU.is_lt))
            link(dve.tensor_tensor(place[:], rank[:], inside[:], ALU.mult))
            link(dve.tensor_reduce(last_rank[:], place[:], AX_X, ALU.max))
            dve.tensor_scalar(room[:], last_rank[:], -1.0, float(CAP), ALU.mult, ALU.add)
            link(dve.tensor_scalar(at_edge[:], rank[:], last_rank[:, 0:1], None, ALU.is_equal))
            link(dve.tensor_tensor_scan(place[:], ones_row[:], at_edge[:], 0.0, ALU.mult, ALU.add))
            link(dve.tensor_tensor(place[:], place[:], at_edge[:], ALU.mult))
            dve.scalar_tensor_tensor(chosen[:], place[:], room[:, 0:1], inside[:], ALU.is_le, ALU.mult)\
               .then_inc(chosen_ready, 1)

            dve.wait_ge(turned, 4 * NT)
            for b in range(B):
                tok = slice(b * SEQ, (b + 1) * SEQ)
                dve.wait_ge(coef_psum, b + 1)
                dve.tensor_tensor(x_a[:, tok], x_a[:, tok], psum[:, b, 0:SEQ], ALU.mult)
                dve.tensor_tensor(x_b[:, tok], x_b[:, tok], psum[0:D2 + 1, 2 + b, 0:SEQ], ALU.mult).then_inc(hin_ready, 1)
            dve.wait_ge(chosen_psum, 1)
            for b in range(B):
                picked = psum[:, 6, 0:TB * B * E].rearrange("p (q b e) -> p q b e", b=B, e=E)[:, :, b, :]
                last = dve.tensor_tensor(weight[:, TB * b:TB * (b + 1), :], gate[:, TB * b:TB * (b + 1), :], picked, ALU.mult)
            link(last)
            for e in range(E - 2, -1, -1):
                link(dve.tensor_tensor(weight[:, :, e], weight[:, :, e], weight[:, :, e + 1], ALU.add))
            for e in range(E):
                n = BLOCKS[e + 1] - BLOCKS[e]
                last = dve.tensor_copy(weight_d[:, :, BLOCKS[e]:BLOCKS[e + 1]],
                                       weight[:, :, e:e + 1].to_broadcast([P, NT, n]))
            last.then_inc(weight_ready, 1)
            project(1)
            attention(1)

            for t in range(NT):
                dve.wait_ge(fc2_done, t + 1)
                link(dve.tensor_tensor(z[:, t, :], psum[:, 2 + t % 2, 0:D], weight_d[:, t, :], ALU.mult))
                dve.tensor_tensor(z[:, t, :], z[:, t, :], acc[:, t, :], ALU.add).then_inc(z_ready, 1)


def kernel(x, txt, L0_tok_W0, L0_tok_b0, L0_tok_W1, L0_tok_b1, L0_tok_W2, L0_tok_b2, L0_tok_Wf, L0_tok_bf,
           L0_tok_idx0, L0_tok_idx1, L0_tok_idx2, L0_attn_w_qkv, L0_attn_b_qkv, L0_attn_w_out, L0_attn_b_out,
           L0_ffn_w_router, L0_ffn_gamma1, L0_ffn_beta1, L0_ffn_w1, L0_ffn_b1, L0_ffn_w2, L0_ffn_b2):
    import concourse.bacc as bacc
    from concourse.bass_utils import run_bass_kernel_spmd

    a = {k: np.asarray(v) for k, v in locals().items() if k not in ("bacc", "run_bass_kernel_spmd")}
    x = a["x"]

    def patches(p):
        h = IMG // p
        t = x.reshape(B, CH, h, p, h, p).transpose(2, 4, 0, 3, 5, 1)
        return t.reshape(h * h, B * p * p * CH)

    def index(name, shape, order):
        i = a[name].view(np.uint32)
        return i.reshape(shape).transpose(order)

    wide, small = constants()
    bias = lambda w, b: np.concatenate([w, b[None, :]], axis=0)
    arrays = {
        "rows0": patches(1), "rows1": patches(2), "rows2": patches(4),
        "idx0": index("L0_tok_idx0", (2, P, GP), (1, 0, 2)).reshape(P, 32),
        "idx1": index("L0_tok_idx1", (64, 2, 8), (1, 0, 2)).reshape(P, 8),
        "idx2": index("L0_tok_idx2", (16, 8, 2), (1, 0, 2)).reshape(P, 2),
        "w0": a["L0_tok_W0"].T,
        "w1": a["L0_tok_W1"].T.reshape(2, 96, EMBED).transpose(1, 0, 2),
        "w2": a["L0_tok_W2"].T.reshape(8, 96, EMBED).transpose(1, 0, 2),
        "tok_bias": np.stack([a["L0_tok_b0"], a["L0_tok_b1"], a["L0_tok_b2"]], axis=1),
        "wf": a["L0_tok_Wf"].T.reshape(3, EMBED, D).transpose(1, 0, 2),
        "bf": a["L0_tok_bf"][None, :],
        "txt": a["txt"],
        "wqkv": bias(a["L0_attn_w_qkv"], a["L0_attn_b_qkv"]),
        "wout": bias(a["L0_attn_w_out"], a["L0_attn_b_out"]),
        "wr": a["L0_ffn_w_router"].T,
        "gb": np.stack([a["L0_ffn_gamma1"], a["L0_ffn_beta1"]], axis=1),
        "fc1": bias(a["L0_ffn_w1"].T, a["L0_ffn_b1"]),
        "fc2": bias(a["L0_ffn_w2"].T, a["L0_ffn_b2"]),
        "wide": wide, "small": small,
    }
    arrays = {k: np.ascontiguousarray(v) for k, v in arrays.items()}
    nc = bacc.Bacc("TRN2", target_bir_lowering=False, num_devices=1)
    args = [nc.dram_tensor(k, v.shape, mybir.dt.from_np(v.dtype), kind="ExternalInput").ap() for k, v in arrays.items()]
    out = nc.dram_tensor("out", (B, SEQ, D), F32, kind="ExternalOutput").ap()
    early_fusion(nc, *args, out)
    r = run_bass_kernel_spmd(nc, [arrays], core_ids=[0])
    return r.results[0]["out"]
```

```python
from contextlib import ExitStack

import numpy as np

import concourse.bass as bass
from concourse import mybir

F32 = mybir.dt.float32
F32R = mybir.dt.float32r
BF16 = mybir.dt.bfloat16
U32 = mybir.dt.uint32
ALU = mybir.AluOpType
ACT = mybir.ActivationFunctionType
AX_X = mybir.AxisListType.X

P = 128
B = 2
IMG = 64
CH = 3
GP = 16
EMBED = 64
D = 192
D2 = D - P
IMG_TOK = 256
TXT_TOK = 128
SEQ = IMG_TOK + TXT_TOK
TOK = B * SEQ
NT = TOK // P
TB = SEQ // P
H = 12
HD = D // H
SLOT = 64
PAIRS = H // 2
HEADS = B * H
GROUP = 3
GROUPS = HEADS // GROUP
LAG = 2
AHEAD = 6
ROOT_FIRST = 24
LN2_STEP = HEADS - 3
LN3_STEP = HEADS - 1
EARLY = HEADS - AHEAD
GW = GROUP * HD
VN = GW + GROUP
VW = 2 * GW + GROUP
MLP = 4 * D
MT = MLP // P
E = 4
CAP = SEQ // 2
ORDER = (2, 5, 0, 3, 1, 4)
BLOCKS = [0, 24, 48, 96, 192]
KC = MT + 2
MERGE = 512 + E * P + D + 1


def constants():
    def interp(n_in):
        pos = np.clip((np.arange(IMG_TOK) + 0.5) * (n_in / IMG_TOK) - 0.5, 0, n_in - 1)
        i0 = np.floor(pos).astype(int)
        i1 = np.minimum(i0 + 1, n_in - 1)
        w = pos - i0
        a = np.zeros((B, n_in, B, IMG_TOK), np.float32)
        for b in range(B):
            a[b, i0, b, np.arange(IMG_TOK)] += (1.0 - w).astype(np.float32)
            a[b, i1, b, np.arange(IMG_TOK)] += w.astype(np.float32)
        return a.reshape(B * n_in, B * IMG_TOK)

    wide = np.zeros((P, P + 512 + 16), np.float32)
    wide[:, :P] = np.eye(P)
    wide[:, P:P + 512] = interp(64)
    wide[:, P + 512 + 7] = 1.0
    small = np.zeros((P, MERGE + VN), np.float32)
    small[:32, :512] = interp(16)
    small[:VN, MERGE:] = np.eye(VN)
    small[VN:VW, MERGE:MERGE + GW] = np.eye(GW)
    for e in range(E):
        small[[e, E + e, 2 * E + e], 512 + e * P:512 + (e + 1) * P] = 1.0
    at = 512 + E * P
    for e in range(E):
        small[e, at:at + BLOCKS[e + 1]] = 1.0
        small[e, at + D] = 1.0
    return wide, small


def ring_uses():
    uses = []
    for step in range(-AHEAD, HEADS + LAG + 1):
        head = step + AHEAD
        if head < HEADS:
            uses += [("S", head, qt) for qt in range(TB)]
        if 0 < head <= HEADS and head % GROUP == 0:
            uses.append(("M", head // GROUP - 1))
        if step > GROUP + LAG - 1 and (step - LAG) % GROUP == 0:
            uses.append(("O", (step - LAG) // GROUP - 1))
        if 0 <= step - EARLY < TB:
            uses.append(("T", step - EARLY))
        if 0 <= step - EARLY - 1 < TB:
            uses.append(("P", step - EARLY - 1))
    return uses


def turn_order():
    order = [("in", t) for t in range(NT)] + [("A0", t) for t in range(TB)]
    order += [("X", t) for t in range(TB)] + [("Y", t) for t in range(TB)] + [("A0", t) for t in range(TB, NT)]
    order += [("X", t) for t in range(TB, NT)] + [("Y", t) for t in range(TB, NT)]
    return order + [("A1", t) for t in range(NT)]


def pool_low(head):
    return (0, 1) if head < EARLY else (0,)


def low_count(layer, head, by_pool):
    heads = [h for n in range(layer + 1) for h in range(HEADS if n < layer else head + 1)]
    return sum(len(pool_low(h)) if by_pool else TB - len(pool_low(h)) for h in heads)


def early_fusion(nc, rows0, rows1, rows2, idx0, idx1, idx2, w0, w1, w2, tok_bias, wf, bf, txt,
                 wqkv, wout, wr, gb, fc1, fc2, wide, small, out):
    uses = ring_uses()
    use_at = {u: n for n, u in enumerate(uses)}
    turn_at = {u: n for n, u in enumerate(turn_order())}
    with ExitStack() as ctx:
        def sb(name, shape, dt=F32):
            return ctx.enter_context(nc.sbuf_tensor(name, shape, dt))

        def sem(name):
            return ctx.enter_context(nc.semaphore(name))

        psum = ctx.enter_context(nc.psum_tensor("psum", [P, 8, 512], F32))

        wide_sb = sb("wide_sb", [P, P + 512 + 16])
        small_sb = sb("small_sb", [P, MERGE + VN])
        eye = wide_sb[:, 0:P]
        interp1 = wide_sb[:, P:P + 512]
        interp2 = small_sb[0:32, 0:512]
        eye_bf = sb("eye_bf", [P, P], BF16)
        pick_col = sb("pick_col", [P, 15], BF16)
        spread = sb("spread", [3 * E, E, P], BF16)
        masks = sb("masks", [E, D + 1], BF16)
        ix0 = sb("ix0", [P, 32], U32)
        ix1 = sb("ix1", [P, 8], U32)
        ix2 = sb("ix2", [P, 2], U32)
        w0_sb = sb("w0_sb", [48, EMBED])
        w1_sb = sb("w1_sb", [96, 2, EMBED])
        w2_sb = sb("w2_sb", [96, 8, EMBED])
        tok_bias_sb = sb("tok_bias_sb", [EMBED, 3])
        wf_sb = sb("wf_sb", [EMBED, 3, D])
        bf_sb = sb("bf_sb", [P, D])
        wqkv_a = sb("wqkv_a", [P, 3 * D])
        wqkv_b = sb("wqkv_b", [D2 + 1, 3 * D])
        wout_a = sb("wout_a", [P, D])
        wout_b = sb("wout_b", [D2 + 1, D])
        wr_a = sb("wr_a", [P, E])
        wr_b = sb("wr_b", [D2, E])
        gb_a = sb("gb_a", [P, 2])
        gb_b = sb("gb_b", [D2, 2])
        fc1_a = sb("fc1_a", [P, MLP])
        fc1_b = sb("fc1_b", [D2 + 1, MLP])
        fc2_sb = sb("fc2_sb", [P, KC, D])

        gelu = sb("gelu", [P, MT, TOK])
        gat0 = sb("gat0", [P, 32, 6])
        gat1 = sb("gat1", [P, 8, 24])
        gat2 = sb("gat2", [P, 2, 96])
        turned0 = sb("turned0", [48, B, 2, P])
        own0 = sb("own0", [P, 2, B, GP, CH])
        own1 = sb("own1", [P, B, 8, 12])
        own2 = sb("own2", [P, B, 2, 48])
        turned1 = sb("turned1", [96, 2, B, 64])
        turned2 = sb("turned2", [96, 8, B, 16])
        level1 = sb("level1", [P, EMBED])
        level2 = sb("level2", [32, EMBED])
        levels = gelu[0:EMBED, 0:2, :].rearrange("p c n -> p (c n)").rearrange("p (l n) -> p l n", l=3)
        fc2_b = gelu[:, 4:MT, :].rearrange("p c n -> p (c n)").rearrange("p (c d) -> p c d", c=KC)

        hid = sb("hid", [P, NT, D])
        xn = sb("xn", [P, NT, D])
        stats = sb("stats", [P, NT, 6])
        mv = sb("mv", [P, NT, 2])
        var_eps = sb("var_eps", [P, NT])
        rstd = sb("rstd", [P, NT])
        half = sb("half", [P, NT])
        x_a = sb("x_a", [P, TOK])
        x_b = sb("x_b", [D2 + 1, TOK])
        nat_q = sb("nat_q", [P, 2, H, SLOT])
        nat_k = sb("nat_k", [P, 2, H, SLOT])
        q_t = sb("q_t", [P, PAIRS, TOK], F32R)
        k_t = sb("k_t", [P, PAIRS, TOK], F32R)
        v_sb = sb("v_sb", [P, NT, H, VW + 1], F32R)
        merge = small_sb[0:VW, MERGE:MERGE + VN]
        neg_max = sb("neg_max", [P, 3, TB, GROUP])
        max_row = sb("max_row", [GROUP, 2, SEQ], F32R)
        prob = sb("prob", [P, 2, TB, SEQ])
        prob_high = sb("prob_high", [P, 3, TB, SEQ], F32R)
        prob_low = sb("prob_low", [P, 3, TB, SEQ], F32R)
        out_t = sb("out_t", [VW, 2, SEQ])
        den = sb("den", [P, 2, TB, GROUP])
        att = sb("att", [P, NT, D])
        att_a = sb("att_a", [P, TOK])
        att_b = sb("att_b", [D2 + 1, TOK])

        y0 = att
        xf_a, xf_b = att_a, att_b
        top = sb("top", [P, NT])
        gate = sb("gate", [P, NT, E])
        gsum = sb("gsum", [P, NT])
        part = sb("part", [P, NT, 3, E], BF16)
        rest = sb("rest", [P, NT, 2, E])
        gate_rows = sb("gate_rows", [3 * E, NT, P], BF16)
        ones_row = prob[0:E, 1, 2, :]
        beats = prob[:, 0, 0:2, :].bitcast(BF16).rearrange("p a (b n) -> p (a b) n", n=SEQ)
        inside = prob[0:E, 0, 1, :]
        last_rank = sb("last_rank", [E, 1])
        room = sb("room", [E, 1])
        at_edge = prob[0:E, 0, 2, :]
        place = prob[0:E, 1, 0, :]
        chosen = sb("chosen", [E, SEQ], BF16)
        weight = sb("weight", [P, NT, E])
        weight_d = xn
        acc = hid
        mlp = y0
        gate_all = gelu[:, 0:E, :].rearrange("p c (b n) -> p b c n", b=B)
        z = y0

        in_idx = sem("in_idx")
        in_wide = sem("in_wide")
        in_tok = sem("in_tok")
        in_txt = sem("in_txt")
        in_qkv = sem("in_qkv")
        in_out = sem("in_out")
        in_fc1 = sem("in_fc1")
        in_fc2 = sem("in_fc2")
        got1 = sem("got1")
        got2 = sem("got2")
        got0 = [sem(f"got0_{part}") for part in range(2)]
        consts_ready = sem("consts_ready")
        v_zeroed = sem("v_zeroed")
        apart = sem("apart")
        pe_tok = sem("pe_tok")
        ev_tok = sem("ev_tok")
        ev_level = sem("ev_level")
        dve_done = sem("dve_done")
        mv_ready = sem("mv_ready")
        rstd_ready = sem("rstd_ready")
        xn_ready = sem("xn_ready")
        y_ready = sem("y_ready")
        pe_turn = sem("pe_turn")
        turned = sem("turned")
        qkv_done = sem("qkv_done")
        high_ready = sem("high_ready")
        low_ready = sem("low_ready")
        stack_psum = sem("stack_psum")
        stack_ready = sem("stack_ready")
        stack_ready_v = sem("stack_ready_v")
        s1_done = sem("s1_done")
        max_ready = sem("max_ready")
        rows_psum = sem("rows_psum")
        rows_ready = sem("rows_ready")
        rows_in = [[sem(f"rows_in_{n}_{layer}") for n in range(GROUPS)] for layer in range(2)]
        s2_done = sem("s2_done")
        exp_ready = sem("exp_ready")
        high_probs = sem("high_probs")
        low_probs_v = sem("low_probs_v")
        low_probs_p = sem("low_probs_p")
        av_done = sem("av_done")
        out_t_ready = sem("out_t_ready")
        out_done = sem("out_done")
        norm_ready = sem("norm_ready")
        proj_done = sem("proj_done")
        hid_ready = sem("hid_ready")
        logits_done = sem("logits_done")
        logits_in = sem("logits_in")
        exp4_ready = sem("exp4_ready")
        parts_ready = sem("parts_ready")
        parts_psum = sem("parts_psum")
        gate_rows_ready = sem("gate_rows_ready")
        spread_done = sem("spread_done")
        gate_all_ready = sem("gate_all_ready")
        beats_ready = sem("beats_ready")
        counted = sem("counted")
        chosen_ready = sem("chosen_ready")
        chosen_psum = sem("chosen_psum")
        coef_psum = sem("coef_psum")
        hin_ready = sem("hin_ready")
        fc1_done = sem("fc1_done")
        gelu_ready = sem("gelu_ready")
        weight_ready = sem("weight_ready")
        mlp_done = sem("mlp_done")
        mlp_copied = sem("mlp_copied")
        mlp_weighted = sem("mlp_weighted")
        mlp_added = sem("mlp_added")
        fc2_done = sem("fc2_done")
        z_ready = sem("z_ready")
        stored = sem("stored")

        block = ctx.enter_context(nc.Block())

        def s1_count(layer, head, qt):
            return layer * HEADS * TB + head * TB + qt + 1

        @block.sync
        def _(sp):
            sp.dma_start(ix1[:], idx1).then_inc(in_idx, 16)
            sp.dma_start(ix2[:], idx2).then_inc(in_idx, 16)
            sp.dma_start(ix0[:], idx0).then_inc(in_idx, 16)
            for b in range(B):
                sp.dma_start(hid[:, TB * b + TB - 1, :], txt[b]).then_inc(in_txt, 16)
            sp.dma_start(wide_sb[:], wide).then_inc(in_wide, 16)
            sp.dma_start(wqkv_a[:], wqkv[0:P]).then_inc(in_qkv, 16)
            sp.dma_start(wqkv_b[:], wqkv[P:]).then_inc(in_qkv, 16)
            for dst, src in ((small_sb, small), (w1_sb, w1), (w2_sb, w2), (w0_sb, w0),
                             (tok_bias_sb, tok_bias), (wf_sb, wf)):
                sp.dma_start(dst[:], src).then_inc(in_tok, 16)
            sp.dma_start(bf_sb[:], bf[0:1, :].to_broadcast([P, D])).then_inc(in_tok, 16)
            sp.dma_start(wout_a[:], wout[0:P]).then_inc(in_out, 16)
            sp.dma_start(wout_b[:], wout[P:]).then_inc(in_out, 16)
            sp.dma_start(wr_a[:], wr[0:P]).then_inc(in_out, 16)
            sp.dma_start(wr_b[:], wr[P:]).then_inc(in_out, 16)
            sp.dma_start(gb_a[:], gb[0:P]).then_inc(in_out, 16)
            sp.dma_start(gb_b[:], gb[P:]).then_inc(in_out, 16)
            sp.dma_start(fc1_a[:], fc1[0:P, 0:MLP]).then_inc(in_fc1, 16)
            sp.dma_start(fc1_b[:], fc1[P:, 0:MLP]).then_inc(in_fc1, 16)
            for half, dst in enumerate((fc2_sb, fc2_b)):
                cols = slice(half * D, (half + 1) * D)
                sp.dma_start(dst[:, 0:KC - 1, :], fc2[0:(KC - 1) * P, cols].rearrange("(c p) d -> p c d", p=P)).then_inc(in_fc2, 16)
                sp.dma_start(dst[0:D2 + 1, KC - 1, :], fc2[(KC - 1) * P:, cols]).then_inc(in_fc2, 16)

            sp.wait_ge(qkv_done, NT)
            sp.dma_start(wqkv_a[:], fc1[0:P, MLP:]).then_inc(in_qkv, 16)
            sp.dma_start(wqkv_b[:], fc1[P:, MLP:]).then_inc(in_qkv, 16)

            for layer in range(2):
                for g in range(GROUPS):
                    sp.wait_ge(rows_ready, layer * GROUPS + g + 1)
                    for n in range(GROUP):
                        b, h = divmod(g * GROUP + n, H)
                        at = SLOT * (h % 2) + 3 * HD
                        sp.dma_start(q_t[at:at + 1, h // 2, b * SEQ:(b + 1) * SEQ].bitcast(F32),
                                     max_row[n:n + 1, g % 2, :].bitcast(F32)).then_inc(rows_in[layer][g], 16)
            for t in range(NT):
                b, p = divmod(t, TB)
                sp.wait_ge(z_ready, t + 1)
                sp.dma_start(out[b, p * P:(p + 1) * P, :], z[:, t, :]).then_inc(stored, 16)
            sp.wait_ge(stored, 16 * NT)

        def low_probs(engine, layer, head, kt, done):
            engine.wait_ge(high_probs, layer * HEADS + head + 1)
            if layer * HEADS + head >= 3:
                engine.wait_ge(av_done, layer * HEADS + head - 2)
            engine.tensor_tensor(prob_low[:, head % 3, kt, :], prob[:, head % 2, kt, :],
                                 prob_high[:, head % 3, kt, :].bitcast(F32), ALU.subtract).then_inc(done, 1)

        @block.gpsimd
        def _(pool):
            pool.wait_ge(in_idx, 48)

            def gather(dst, rows, index, done):
                nc.gpsimd.indirect_dma_start(
                    out=dst, out_offset=None, in_=rows,
                    in_offset=bass.IndirectOffsetOnAxis(ap=index, axis=0)).then_inc(done, 16)

            def root(n, tiles):
                pool.wait_ge(mv_ready, n + 1)
                pool.tensor_tensor(rstd[:, tiles], var_eps[:, tiles], half[:, tiles], ALU.pow).then_inc(rstd_ready, 1)

            for j in range(8):
                gather(gat1[:, j, :], rows1, ix1[:, j:j + 1], got1)
            root(0, slice(2, NT, TB))
            for j in range(2):
                gather(gat2[:, j, :], rows2, ix2[:, j:j + 1], got2)
            for j in range(32):
                gather(gat0[:, j, :], rows0, ix0[:, j:j + 1], got0[j // GP])
                if j == ROOT_FIRST:
                    root(1, slice(0, NT, TB))
            root(2, slice(1, NT, TB))
            for layer in range(2):
                if layer == 1:
                    pool.wait_ge(weight_ready, B)
                    for t in range(NT):
                        pool.wait_ge(mlp_copied, t + 1)
                        pool.tensor_tensor(mlp[:, t, :], mlp[:, t, :], weight_d[:, t, :], ALU.mult).then_inc(mlp_weighted, 1)
                        pool.wait_ge(mlp_weighted, t + 1)
                        pool.tensor_tensor(acc[:, t, :], acc[:, t, :], mlp[:, t, :], ALU.add).then_inc(mlp_added, 1)
                for head in range(HEADS):
                    for kt in pool_low(head):
                        low_probs(pool, layer, head, kt, low_probs_p)
                    if layer == 0 and head in (LN2_STEP, LN3_STEP):
                        root(3 + (head == LN3_STEP), slice(0, TB))
                if layer == 0:
                    root(5, slice(TB, NT))
                    root(6, slice(TB, NT))

        @block.tensor
        def _(pe):
            mm = nc.tensor.matmul

            def coarse_levels():
                for done, n in ((high_ready, 4), (low_ready, 2), (stack_ready, 4), (stack_ready_v, 2)):
                    pe.wait_ge(done, n)
                pe.wait_ge(in_tok, 112)
                pe.wait_ge(apart, 1)
                for b in range(B):
                    last = nc.tensor.transpose(psum[0:96, 0, b * P:(b + 1) * P], own1[:, b].rearrange("p j c -> p (j c)"), eye)
                last.then_inc(pe_tok, 1)
                pe.wait_ge(apart, 2)
                for b in range(B):
                    last = nc.tensor.transpose(psum[0:96, 1, b * P:(b + 1) * P], own2[:, b].rearrange("p j c -> p (j c)"), eye)
                last.then_inc(pe_tok, 1)
                pe.wait_ge(ev_tok, 1)
                for jh in range(2):
                    last = mm(psum[:, 2, 0:EMBED], turned1[:, jh].rearrange("p b g -> p (b g)"), w1_sb[:, jh, :],
                              start=jh == 0, stop=jh == 1)
                last.then_inc(pe_tok, 1)
                pe.wait_ge(ev_tok, 2)
                for jh in range(8):
                    last = mm(psum[0:32, 3, 0:EMBED], turned2[:, jh].rearrange("p b g -> p (b g)"), w2_sb[:, jh, :],
                              start=jh == 0, stop=jh == 7)
                last.then_inc(pe_tok, 1)
                pe.wait_ge(ev_tok, 3)
                mm(psum[0:EMBED, 4, :], level1[:], interp1, start=True, stop=True).then_inc(pe_tok, 1)
                pe.wait_ge(ev_tok, 4)
                mm(psum[0:EMBED, 5, :], level2[:], interp2, start=True, stop=True).then_inc(pe_tok, 1)

            def image_part(gt):
                done = 2 * (gt + 1)
                pe.wait_ge(apart, 3 + gt)
                pe.wait_ge(stack_ready_v, done)
                for b in range(B):
                    last = nc.tensor.transpose(psum[0:48, 6, b * P:(b + 1) * P],
                                               own0[:, gt, b].rearrange("p j c -> p (j c)"), eye)
                last.then_inc(pe_tok, 1)
                pe.wait_ge(ev_level, 3 + 2 * gt)
                pe.wait_ge(stack_ready, 2 * done)
                mm(psum[0:EMBED, 7, 0:B * P], w0_sb[:], turned0[:, :, gt, :], start=True, stop=True).then_inc(pe_tok, 1)
                pe.wait_ge(ev_level, 4 + 2 * gt)
                pe.wait_ge(high_ready, 2 * done)
                pe.wait_ge(low_ready, done)
                for b in range(B):
                    n = 2 * b + gt
                    for lv in range(3):
                        last = mm(psum[:, b, 0:D], levels[:, lv, n * P:(n + 1) * P], wf_sb[:, lv, :],
                                  start=lv == 0, stop=lv == 2)
                    last.then_inc(pe_tok, 1)

            def turn(src, t, bank, done):
                nc.tensor.transpose(psum[:, bank, 0:P], src[:, t, 0:P], eye)
                nc.tensor.transpose(psum[0:D2, bank, P:2 * P], src[:, t, P:D], eye).then_inc(done, 1)

            def project(layer, first, end):
                wa, wb, at = wqkv_a, wqkv_b, 0

                def stack_copied(n, u):
                    if u == 1:
                        pe.wait_ge(stack_ready_v, n + 1)
                    else:
                        pe.wait_ge(stack_ready, 2 * n + (u > 0) + 1)

                def stacks(t):
                    pe.wait_ge(high_ready, 2 * (layer * NT + t + 1))
                    pe.wait_ge(low_ready, layer * NT + t + 1)
                    for u in range(3):
                        if layer * NT + t >= 1:
                            stack_copied(layer * NT + t - 1, u)
                        for i in range(4):
                            c = 4 * u + i
                            nat = (nat_q, nat_k)[c // PAIRS]
                            pair = c % PAIRS
                            last = nc.tensor.transpose(
                                psum[:, 5 + u, i * P:(i + 1) * P],
                                nat[:, t % 2, 2 * pair:2 * pair + 2, :], eye)
                        last.then_inc(stack_psum, 1)

                def turn_input(t):
                    pe.wait_ge(xn_ready, t + 1)
                    if t >= 1:
                        pe.wait_ge(turned, t)
                    turn(xn, ORDER[t], 4, pe_turn)

                if layer == 0:
                    turn_input(first)
                for t in range(first, end):
                    if layer == 0:
                        if t + 1 < end:
                            turn_input(t + 1)
                        pe.wait_ge(turned, t + 1)
                    else:
                        pe.wait_ge(hin_ready, t // TB + 1)
                    if t >= 2:
                        pe.wait_ge(high_ready, 2 * (layer * NT + t - 1))
                        pe.wait_ge(low_ready, layer * NT + t - 1)
                    tile = ORDER[t] if layer == 0 else t
                    tok = slice(tile * P, (tile + 1) * P)
                    for bank, w in ((2 * (t % 2), slice(at, at + 2 * D)),
                                    (2 * (t % 2) + 1, slice(at + 2 * D, at + 3 * D))):
                        n = w.stop - w.start
                        mm(psum[:, bank, 0:n], x_a[:, tok], wa[:, w], start=True, stop=False)
                        last = mm(psum[:, bank, 0:n], x_b[:, tok], wb[:, w], start=False, stop=True)
                    last.then_inc(qkv_done, 1)
                    if layer == 1 and t == 1:
                        coefficients(1, 6)
                        for f in range(MT):
                            feed_forward_up(1, f)
                            if f == 0:
                                turn_chosen()
                        pe.wait_ge(weight_ready, B)
                        pe.wait_ge(gelu_ready, B * MT)
                    if t > first:
                        stacks(t - 1)
                stacks(end - 1)

            def keep_clock(bank):
                mm(psum[:, bank, 0:256], eye, wide_sb[:, 0:256], start=True, stop=True)

            def feed_forward_down(t, third):
                pe.wait_ge(gelu_ready, B * MT)
                if t >= 2:
                    pe.wait_ge(mlp_copied, t - 1)
                for c in range(third * MT // TB, (third + 1) * MT // TB):
                    last = mm(psum[:, 6 + t % 2, 0:D], gelu[:, c, t * P:(t + 1) * P], fc2_sb[:, c, :],
                              start=c == 0, stop=c == MT - 1)
                if third == TB - 1:
                    last.then_inc(mlp_done, 1)

            def turn_next(src, kind, t):
                n = turn_at[kind, t]
                if kind == "X":
                    pe.wait_ge(xn_ready, NT + t + 1)
                if kind == "Y":
                    pe.wait_ge(y_ready, t + 1)
                if n - 4 >= turn_at["A0", 0]:
                    pe.wait_ge(turned, n - 3)
                turn(src, t, 2 + n % 4, pe_turn)

            def logits(b):
                for t in range(b * TB, (b + 1) * TB):
                    pe.wait_ge(turned, turn_at["X", t] + 1)
                    tok = slice(t * P, (t + 1) * P)
                    mm(psum[:, 6 + b, t * E:(t + 1) * E], xf_a[:, tok], wr_a[:], start=True, stop=False)
                    last = mm(psum[:, 6 + b, t * E:(t + 1) * E], xf_b[0:D2, tok], wr_b[:], start=False, stop=True)
                last.then_inc(logits_done, 1)

            def gates_to_rows(b):
                pe.wait_ge(parts_ready, b + 1)
                for t in range(TB):
                    last = nc.tensor.transpose(
                        psum[0:3 * E, 7, t * (P // 2):(t + 1) * (P // 2)].bitcast(BF16),
                        part[:, b * TB + t].rearrange("p a e -> p (a e)"), eye_bf[:])
                last.then_inc(parts_psum, 1)

            def spread_gates(b):
                pe.wait_ge(gate_rows_ready, b + 1)
                for e in range(E):
                    n = b * E + e
                    if e >= 2:
                        pe.wait_ge(gate_all_ready, n - 1)
                    mm(psum[:, e % 2, 0:SEQ], spread[:, e, :], gate_rows[:, TB * b:TB * (b + 1), :],
                       start=True, stop=True).then_inc(spread_done, 1)

            def count(b, n):
                pe.wait_ge(beats_ready, b * E * TB + n + 1)
                e = n // TB
                mm(psum[0:E, 6, 0:SEQ], pick_col[:, 7 - e:7 - e + E], beats[:, n % 4, :],
                   start=n == 0, stop=n == E * TB - 1).then_inc(counted, 1)

            def coefficients(b, bank):
                pe.wait_ge(chosen_ready, b + 1)
                mm(psum[:, bank, 0:SEQ], masks[:, 0:P], chosen[:], start=True, stop=True)
                mm(psum[0:D2 + 1, bank + 1, 0:SEQ], masks[:, P:D + 1], chosen[:],
                   start=True, stop=True).then_inc(coef_psum, 1)

            def turn_chosen():
                for p in range(TB):
                    last = mm(psum[:, 6, p * E:(p + 1) * E], chosen[:, p * P:(p + 1) * P], eye_bf[0:E, 0:E],
                              start=True, stop=True)
                last.then_inc(chosen_psum, 1)

            def feed_forward_up(b, f):
                n = b * MT + f
                pe.wait_ge(hin_ready, b + 1)
                if n >= 2:
                    pe.wait_ge(gelu_ready, n - 1)
                tok = slice(b * SEQ, (b + 1) * SEQ)
                mm(psum[:, 4 + n % 2, 0:SEQ], fc1_a[:, f * P:(f + 1) * P], x_a[:, tok], start=True, stop=False)
                mm(psum[:, 4 + n % 2, 0:SEQ], fc1_b[:, f * P:(f + 1) * P], x_b[:, tok],
                   start=False, stop=True).then_inc(fc1_done, 1)

            def attention(layer):
                def free_ring_bank(n):
                    if n < 2:
                        return
                    if uses[n - 2][0] == "S":
                        pe.wait_ge(max_ready, s1_count(layer, uses[n - 2][1], uses[n - 2][2]))
                    elif uses[n - 2][0] == "O":
                        pe.wait_ge(norm_ready, layer * GROUPS + uses[n - 2][1] + 1)
                    elif uses[n - 2][0] == "T":
                        pe.wait_ge(turned, turn_at[f"A{layer}", uses[n - 2][1]] + 1)
                    elif uses[n - 2][0] == "P":
                        pe.wait_ge((hid_ready, z_ready)[layer], uses[n - 2][1] + 1)
                    else:
                        pe.wait_ge(rows_ready, layer * GROUPS + uses[n - 2][1] + 1)

                def scores_for_max(head, qt):
                    b, h = divmod(head, H)
                    rows = slice(SLOT * (h % 2), SLOT * (h % 2) + 3 * HD)
                    n = use_at[("S", head, qt)]
                    free_ring_bank(n)
                    mm(psum[:, n % 2, 0:SEQ], q_t[rows, h // 2, b * SEQ + qt * P:b * SEQ + (qt + 1) * P],
                       k_t[rows, h // 2, b * SEQ:(b + 1) * SEQ], start=True, stop=True).then_inc(s1_done, 1)

                def turn_maxima(g):
                    n = use_at[("M", g)]
                    free_ring_bank(n)
                    pe.wait_ge(max_ready, s1_count(layer, g * GROUP + GROUP - 1, TB - 1))
                    for qt in range(TB):
                        last = nc.tensor.transpose(psum[0:GROUP, n % 2, qt * P:(qt + 1) * P],
                                                   neg_max[:, g % 3, qt, :], eye)
                    last.then_inc(rows_psum, 1)

                def scores_for_exp(head):
                    b, h = divmod(head, H)
                    rows = slice(SLOT * (h % 2), SLOT * (h % 2) + 3 * HD + 1)
                    if head % GROUP == 0:
                        pe.wait_ge(rows_in[layer][head // GROUP], 16 * GROUP)
                    for kt in range(TB):
                        n = layer * HEADS * TB + head * TB + kt
                        if n >= 4:
                            pe.wait_ge(exp_ready, n - 3)
                        mm(psum[:, 2 + n % 4, 0:SEQ], k_t[rows, h // 2, b * SEQ + kt * P:b * SEQ + (kt + 1) * P],
                           q_t[rows, h // 2, b * SEQ:(b + 1) * SEQ], start=True, stop=True).then_inc(s2_done, 1)

                def weigh_values(head, kt):
                    b, h = divmod(head, H)
                    g, hl = divmod(head, GROUP)
                    if hl == 0 and kt == 0 and g >= 2:
                        pe.wait_ge(out_t_ready, layer * GROUPS + g - 1)
                    elif hl == 0 and kt == 0 and layer == 1:
                        pe.wait_ge(mlp_copied, NT)
                    pe.wait_ge(high_probs, layer * HEADS + head + 1)
                    mm(psum[0:VW, 6 + g % 2, 0:SEQ], v_sb[:, TB * b + kt, h, 0:VW], prob_high[:, head % 3, kt, :],
                       start=hl == 0 and kt == 0, stop=False)
                    pooled = kt in pool_low(head)
                    later = (len(pool_low(head)) if pooled else TB) - kt - 1
                    pe.wait_ge(low_probs_p if pooled else low_probs_v, low_count(layer, head, pooled) - later)
                    last = mm(psum[0:VW, 6 + g % 2, 0:SEQ], v_sb[:, TB * b + kt, h, 0:VW], prob_low[:, head % 3, kt, :],
                              start=False, stop=hl == GROUP - 1 and kt == TB - 1)
                    if kt == TB - 1:
                        last.then_inc(av_done, 1)

                def turn_output(g):
                    n = use_at[("O", g)]
                    free_ring_bank(n)
                    pe.wait_ge(out_t_ready, layer * GROUPS + g + 1)
                    for qt in range(TB):
                        last = mm(psum[:, n % 2, qt * VN:(qt + 1) * VN], out_t[:, g % 2, qt * P:(qt + 1) * P], merge,
                                  start=True, stop=True)
                    last.then_inc(out_done, 1)

                def project_output(t, bank):
                    w_a, w_b, done = ((wout_a[:], wout_b[:], proj_done),
                                      (fc2_sb[:, MT, :], fc2_sb[0:D2 + 1, MT + 1, :], fc2_done))[layer]
                    tok = slice(t * P, (t + 1) * P)
                    pe.wait_ge(turned, turn_at[f"A{layer}", t] + 1)
                    mm(psum[:, bank, 0:D], att_a[:, tok], w_a, start=True, stop=False)
                    mm(psum[:, bank, 0:D], att_b[:, tok], w_b, start=False, stop=True).then_inc(done, 1)

                pe.wait_ge(stack_ready, 2 * NT * (layer + 1))
                pe.wait_ge(stack_ready_v, NT * (layer + 1))
                for step in range(-AHEAD, HEADS + LAG + 1):
                    if 0 <= step < HEADS:
                        scores_for_exp(step)
                    head = step + AHEAD
                    for n in range(TB):
                        if head < HEADS:
                            scores_for_max(head, n)
                        if layer == 0 and step < LAG:
                            keep_clock(7)
                        if layer == 1 and LAG - NT <= step < LAG:
                            feed_forward_down(step + NT - LAG, n)
                        if LAG <= step < HEADS + LAG:
                            weigh_values(step - LAG, n)
                    if 0 < head <= HEADS and head % GROUP == 0:
                        turn_maxima(head // GROUP - 1)
                    if step > GROUP + LAG - 1 and (step - LAG) % GROUP == 0:
                        turn_output((step - LAG) // GROUP - 1)
                    t = step - EARLY
                    if 0 <= t < TB:
                        n = use_at[("T", t)]
                        free_ring_bank(n)
                        pe.wait_ge(norm_ready, layer * GROUPS + GROUPS // B)
                        turn(att, t, n % 2, pe_turn)
                    if 0 <= t - 1 < TB:
                        n = use_at[("P", t - 1)]
                        free_ring_bank(n)
                        project_output(t - 1, n % 2)

                pe.wait_ge(exp_ready, (layer + 1) * HEADS * TB)
                if layer == 0:
                    for t in range(TB):
                        turn_next(xn, "X", t)
                    for t in range(TB):
                        turn_next(y0, "Y", t)
                    logits(0)
                pe.wait_ge(norm_ready, GROUPS * (layer + 1))
                turn_next(att, f"A{layer}", TB)
                for t in range(TB, NT):
                    if t + 1 < NT:
                        turn_next(att, f"A{layer}", t + 1)
                    if t >= TB + 2:
                        pe.wait_ge((hid_ready, z_ready)[layer], t - 1)
                    project_output(t, t % 2)

            pe.wait_ge(in_qkv, 32)
            pe.wait_ge(in_wide, 16)
            project(0, 0, 2)
            coarse_levels()
            image_part(0)
            for n in range(6):
                keep_clock(4)
            project(0, 2, 4)
            image_part(1)
            for n in range(6):
                keep_clock(4)
            project(0, 4, 6)
            pe.wait_ge(in_out, 96)
            attention(0)

            gates_to_rows(0)
            pe.wait_ge(hid_ready, NT)
            spread_gates(0)
            for n in range(E * TB):
                count(0, n)
            for t in range(TB, NT):
                turn_next(xn, "X", t)
            logits(1)
            pe.wait_ge(gate_all_ready, E)
            for n in range(8):
                keep_clock(0)
            coefficients(0, 0)
            turn_chosen()
            for t in range(TB, NT):
                turn_next(y0, "Y", t)
            pe.wait_ge(in_fc1, 32)
            pe.wait_ge(turned, turn_at["Y", NT - 1] + 1)
            for f in range(MT):
                feed_forward_up(0, f)
                if f == 0:
                    gates_to_rows(1)
                if f == 1:
                    spread_gates(1)
                if f >= MT - E:
                    for n in range(TB):
                        count(1, TB * (f - MT + E) + n)

            pe.wait_ge(in_qkv, 64)
            project(1, 0, NT)
            attention(1)

        @block.scalar
        def _(act):
            def coarse_levels():
                act.wait_ge(pe_tok, 5)
                act.wait_ge(in_tok, 112)
                act.activation(levels[:, 1, :], psum[0:EMBED, 4, :], ACT.Identity, bias=tok_bias_sb[:, 1:2]).then_inc(ev_level, 1)
                act.wait_ge(pe_tok, 6)
                act.activation(levels[:, 2, :], psum[0:EMBED, 5, :], ACT.Identity, bias=tok_bias_sb[:, 2:3]).then_inc(ev_level, 1)

            def image_part(gt):
                act.wait_ge(pe_tok, 7 + 4 * gt)
                act.activation(turned0[:, :, gt, :], psum[0:48, 6, 0:B * P].rearrange("p (b n) -> p b n", b=B),
                               ACT.Copy).then_inc(ev_level, 1)
                act.wait_ge(pe_tok, 8 + 4 * gt)
                act.activation(levels[:, 0, :].rearrange("p (b g n) -> p b g n", b=B, g=2)[:, :, gt, :],
                               psum[0:EMBED, 7, 0:B * P].rearrange("p (b n) -> p b n", b=B),
                               ACT.Identity, bias=tok_bias_sb[:, 0:1]).then_inc(ev_level, 1)

            def copy_turned(kind, t, bank, dst_a, dst_b):
                tile = ORDER[t] if kind == "in" else t
                tok = slice(tile * P, (tile + 1) * P)
                act.wait_ge(pe_turn, turn_at[kind, t] + 1)
                act.activation(dst_a[:, tok], psum[:, bank, 0:P], ACT.Copy)
                act.activation(dst_b[0:D2, tok], psum[0:D2, bank, P:2 * P], ACT.Copy).then_inc(turned, 1)

            def copy_expert_input(t):
                tok = slice(t * P, (t + 1) * P)
                n = turn_at["Y", t]
                act.wait_ge(pe_turn, n + 1)
                act.activation(x_a[:, tok], psum[:, 2 + n % 4, 0:P], ACT.Identity, scale=gb_a[:, 0:1], bias=gb_a[:, 1:2])
                act.activation(x_b[0:D2, tok], psum[0:D2, 2 + n % 4, P:2 * P], ACT.Identity,
                               scale=gb_b[:, 0:1], bias=gb_b[:, 1:2]).then_inc(turned, 1)

            def exp_logits(b):
                act.wait_ge(logits_in, b + 1)
                g = gate[:, b * TB:(b + 1) * TB]
                act.activation(g, g, ACT.Exp).then_inc(exp4_ready, 1)

            def copy_gate_rows(b):
                act.wait_ge(parts_psum, b + 1)
                act.activation(gate_rows[:, b * TB:(b + 1) * TB],
                               psum[0:3 * E, 7, 0:TB * P // 2].bitcast(BF16).rearrange("p (t b) -> p t b", b=P),
                               ACT.Copy).then_inc(gate_rows_ready, 1)

            def copy_gate_all(b):
                for e in range(E):
                    act.wait_ge(spread_done, b * E + e + 1)
                    act.activation(gate_all[:, b, e, :], psum[:, e % 2, 0:SEQ], ACT.Copy).then_inc(gate_all_ready, 1)

            def gelus(b, f):
                n = b * MT + f
                act.wait_ge(fc1_done, n + 1)
                act.activation(gelu[:, f, b * SEQ:(b + 1) * SEQ], psum[:, 4 + n % 2, 0:SEQ], ACT.Gelu).then_inc(gelu_ready, 1)

            def stacks(layer, t):
                tile = ORDER[t] if layer == 0 else t
                for u in (0, 2):
                    n = 3 * (layer * NT + t) + u
                    act.wait_ge(stack_psum, n + 1)
                    pair = 0 if u == 0 else 2
                    act.activation((q_t if u == 0 else k_t)[:, pair:pair + 4, tile * P:(tile + 1) * P],
                                   psum[:, 5 + u, :].rearrange("p (a b) -> p a b", b=P), ACT.Copy).then_inc(stack_ready, 1)

            def project(layer, first, end):
                if layer == 0:
                    copy_turned("in", first, 4, x_a, x_b)
                for t in range(first, end):
                    if layer == 0 and t + 1 < end:
                        copy_turned("in", t + 1, 4, x_a, x_b)
                    act.wait_ge(qkv_done, layer * NT + t + 1)
                    if t == 0:
                        act.wait_ge(consts_ready, 1)
                    if layer * NT + t >= 2:
                        act.wait_ge(stack_psum, 3 * (layer * NT + t - 1))
                    src = psum[:, 2 * (t % 2), 0:2 * D].rearrange("p (s h d) -> p s h d", s=2, h=H)
                    for s, nat, slots in ((0, nat_q, (0, 2)), (1, nat_k, (0, 1))):
                        dst = nat[:, t % 2].bitcast(F32R)
                        for n, slot in enumerate(slots):
                            last = act.activation(dst[:, :, slot * HD:(slot + 1) * HD], src[:, s], ACT.Copy)
                        last.then_inc(high_ready, 1)
                    if layer == 1 and t == 1:
                        for f in range(MT):
                            gelus(1, f)
                    if t > first:
                        stacks(layer, t - 1)
                stacks(layer, end - 1)

            def attention(layer):
                for step in range(-AHEAD, HEADS + LAG + 1):
                    if 0 <= step < HEADS:
                        for kt in range(TB):
                            n = layer * HEADS * TB + step * TB + kt
                            act.wait_ge(s2_done, n + 1)
                            if layer * HEADS + step >= 2 and kt == 0:
                                before = divmod(layer * HEADS + step - 2, HEADS)
                                act.wait_ge(low_probs_v, low_count(*before, False))
                                act.wait_ge(low_probs_p, low_count(*before, True))
                            act.activation(prob[:, step % 2, kt, :], psum[:, 2 + n % 4, 0:SEQ], ACT.Exp,
                                           scale=float(HD) ** -0.5).then_inc(exp_ready, 1)
                    if step > GROUP + LAG - 1 and (step - LAG) % GROUP == 0:
                        g = (step - LAG) // GROUP - 1
                        act.wait_ge(av_done, layer * HEADS + (g + 1) * GROUP)
                        act.activation(out_t[:, g % 2, :], psum[0:VW, 6 + g % 2, 0:SEQ], ACT.Copy).then_inc(out_t_ready, 1)
                    if 0 <= step < EARLY:
                        act.wait_ge(exp_ready, n + 1)
                        if layer * HEADS + step >= 3:
                            act.wait_ge(av_done, layer * HEADS + step - 2)
                        act.activation(prob_high[:, step % 3], prob[:, step % 2], ACT.Copy).then_inc(high_probs, 1)
                    if layer == 1 and LAG - NT <= step < LAG:
                        t = step + NT - LAG
                        act.wait_ge(mlp_done, t + 1)
                        act.activation(mlp[:, t, :], psum[:, 6 + t % 2, 0:D], ACT.Copy).then_inc(mlp_copied, 1)
                    head = step + AHEAD
                    if 0 < head <= HEADS and head % GROUP == 0:
                        g = head // GROUP - 1
                        act.wait_ge(rows_psum, layer * GROUPS + g + 1)
                        if g >= 2:
                            act.wait_ge(rows_in[layer][g - 2], 16 * GROUP)
                        elif layer:
                            act.wait_ge(rows_in[0][GROUPS - 2 + g], 16 * GROUP)
                        act.activation(max_row[:, g % 2, :], psum[0:GROUP, use_at[("M", g)] % 2, 0:SEQ],
                                       ACT.Copy).then_inc(rows_ready, 1)
                    t = step - EARLY
                    if 0 <= t < TB:
                        copy_turned(f"A{layer}", t, use_at[("T", t)] % 2, att_a, att_b)
                if layer == 0:
                    for t in range(TB):
                        copy_turned("X", t, 2 + turn_at["X", t] % 4, xf_a, xf_b)
                    for t in range(TB):
                        copy_expert_input(t)
                    exp_logits(0)
                for t in range(TB, NT):
                    kind = f"A{layer}"
                    copy_turned(kind, t, 2 + turn_at[kind, t] % 4, att_a, att_b)

            project(0, 0, 2)
            coarse_levels()
            image_part(0)
            project(0, 2, 4)
            image_part(1)
            project(0, 4, 6)
            attention(0)
            copy_gate_rows(0)
            copy_gate_all(0)
            for t in range(TB, NT):
                copy_turned("X", t, 2 + turn_at["X", t] % 4, xf_a, xf_b)
            for t in range(TB, NT):
                copy_expert_input(t)
            exp_logits(1)
            for f in range(MT):
                gelus(0, f)
                if f == 0:
                    copy_gate_rows(1)
                if f == 1:
                    copy_gate_all(1)
            project(1, 0, NT)
            attention(1)

        @block.vector
        def _(dve):
            chain = [0]

            def link(instruction):
                chain[0] += 1
                instruction.then_inc(dve_done, 1)
                dve.wait_ge(dve_done, chain[0])

            dve.memset(half[:], -0.5)
            def add_halves():
                dve.wait_ge(in_fc2, 64)
                dve.tensor_tensor(fc2_sb[:, 0:KC - 1, :], fc2_sb[:, 0:KC - 1, :], fc2_b[:, 0:KC - 1, :], ALU.add)
                link(dve.tensor_tensor(fc2_sb[0:D2 + 1, KC - 1, :], fc2_sb[0:D2 + 1, KC - 1, :],
                                       fc2_b[0:D2 + 1, KC - 1, :], ALU.add))

            def image_part(gt):
                dve.wait_ge(got0[gt], GP * 16)
                dve.tensor_copy(own0[:, gt], gat0[:, GP * gt:GP * (gt + 1), :].rearrange("p j (b c) -> p b j c", b=B))\
                   .then_inc(apart, 1)
                for b in range(B):
                    dve.wait_ge(pe_tok, 9 + 4 * gt + b)
                    last = dve.tensor_tensor(hid[:, TB * b + gt, :], psum[:, b, 0:D], bf_sb[:], ALU.add)
                link(last)
                moments(hid, 1e-5, range(gt, NT, TB))
                normalised(1 + gt, hid, xn, xn_ready, range(gt, NT, TB))

            def moments(src, eps, tiles):
                for t in tiles:
                    last = dve.bn_stats(stats[:, t, :], src[:, t, :])
                link(last)
                for t in tiles:
                    last = dve.bn_aggr(mv[:, t, :], stats[:, t, :])
                link(last)
                span = slice(tiles[0], tiles[-1] + 1, tiles[1] - tiles[0])
                dve.tensor_scalar(var_eps[:, span], mv[:, span, 1], eps, None,
                                  ALU.add).then_inc(mv_ready, 1)

            def normalised(n, src, dst, ready, tiles):
                dve.wait_ge(rstd_ready, n + 1)
                for t in tiles:
                    dve.tensor_scalar(dst[:, t, :], src[:, t, :], mv[:, t, 0:1], rstd[:, t:t + 1],
                                      ALU.subtract, ALU.mult).then_inc(ready, 1)

            def add_residual(t, bank):
                dve.wait_ge(proj_done, t + 1)
                dve.tensor_tensor(hid[:, t, :], psum[:, bank, 0:D], hid[:, t, :], ALU.add).then_inc(hid_ready, 1)

            def second_norm(b):
                tiles = range(b * TB, (b + 1) * TB)
                normalised(3 + 2 * b, hid, xn, xn_ready, tiles)
                dve.wait_ge(xn_ready, NT + (b + 1) * TB)
                dve.tensor_tensor(acc[:, b * TB:(b + 1) * TB], hid[:, b * TB:(b + 1) * TB], xn[:, b * TB:(b + 1) * TB], ALU.add)
                moments(xn, 1e-6, tiles)

            def form_output(t, bank):
                dve.wait_ge(fc2_done, t + 1)
                link(dve.tensor_tensor(z[:, t, :], psum[:, bank, 0:D], weight_d[:, t, :], ALU.mult))
                dve.tensor_tensor(z[:, t, :], z[:, t, :], acc[:, t, :], ALU.add).then_inc(z_ready, 1)

            def middle_stack(layer, t):
                tile = ORDER[t] if layer == 0 else t
                n = 3 * (layer * NT + t) + 1
                dve.wait_ge(stack_psum, n + 1)
                for dst, pair, i in ((q_t, 4, 0), (k_t, 0, 2)):
                    last = dve.tensor_copy(dst[:, pair:pair + 2, tile * P:(tile + 1) * P],
                                           psum[:, 6, i * P:(i + 2) * P].rearrange("p (a b) -> p a b", b=P))
                last.then_inc(stack_ready_v, 1)

            def project(layer, first, end):
                for t in range(first, end):
                    dve.wait_ge(high_ready, 2 * (layer * NT + t + 1))
                    bank = psum[:, 2 * (t % 2), 0:2 * D].rearrange("p (s h d) -> p s h d", s=2, h=H)
                    dve.tensor_tensor(nat_q[:, t % 2, :, HD:2 * HD].bitcast(F32R), bank[:, 0], nat_q[:, t % 2, :, 0:HD], ALU.subtract)
                    dve.tensor_tensor(nat_k[:, t % 2, :, 2 * HD:3 * HD].bitcast(F32R), bank[:, 1], nat_k[:, t % 2, :, 0:HD], ALU.subtract)
                    v = psum[:, 2 * (t % 2) + 1, 0:D].rearrange("p (g h d) -> p g h d", h=GROUP, d=HD)
                    dst = v_sb[:, ORDER[t] if layer == 0 else t].rearrange("p (g h) w -> p g h w", h=GROUP)
                    for hl in range(GROUP):
                        high = dst[:, :, hl, hl * HD:(hl + 1) * HD]
                        last = dve.tensor_copy(high, v[:, :, hl, :])
                    link(last)
                    for hl in range(GROUP):
                        high = dst[:, :, hl, hl * HD:(hl + 1) * HD]
                        last = dve.tensor_tensor(dst[:, :, hl, VN + hl * HD:VN + (hl + 1) * HD], v[:, :, hl, :],
                                                 high.bitcast(F32), ALU.subtract)
                    last.then_inc(low_ready, 1)
                    if t > first:
                        middle_stack(layer, t - 1)
                middle_stack(layer, end - 1)

            def attention(layer):
                def normalise(g):
                    b, h0 = divmod(g * GROUP, H)
                    dve.wait_ge(out_done, layer * GROUPS + g + 1)
                    if layer == 1 and g == 0:
                        dve.wait_ge(mlp_added, NT)
                    o = psum[:, use_at[("O", g)] % 2, 0:TB * VN].rearrange("p (q n) -> p q n", q=TB)
                    link(dve.reciprocal(den[:, g % 2], o[:, :, GW:VN]))
                    dst = att[:, TB * b:TB * (b + 1), h0 * HD:(h0 + GROUP) * HD].rearrange("p q (h d) -> p q h d", h=GROUP)
                    dve.tensor_tensor(dst, o[:, :, 0:GW].rearrange("p q (h d) -> p q h d", h=GROUP),
                                      den[:, g % 2].rearrange("p q (h o) -> p q h o", o=1).to_broadcast([P, TB, GROUP, HD]),
                                      ALU.mult).then_inc(norm_ready, 1)

                for step in range(-AHEAD, HEADS + LAG + 1):
                    head = step + AHEAD
                    if head < HEADS:
                        g, hl = divmod(head, GROUP)
                        for qt in range(TB):
                            if qt == 1 and step >= 1:
                                low_probs(dve, layer, step - 1, TB - 1, low_probs_v)
                            dve.wait_ge(s1_done, s1_count(layer, head, qt))
                            if hl == 0 and qt == 0 and g >= 3:
                                dve.wait_ge(rows_psum, layer * GROUPS + g - 2)
                            dve.tensor_reduce(neg_max[:, g % 3, qt, hl:hl + 1], psum[:, use_at[("S", head, qt)] % 2, 0:SEQ],
                                              AX_X, ALU.max, negate=True).then_inc(max_ready, 1)
                    elif step == EARLY:
                        low_probs(dve, layer, step - 1, TB - 1, low_probs_v)
                    if step > GROUP + LAG - 1 and (step - LAG) % GROUP == 0:
                        normalise((step - LAG) // GROUP - 1)
                    t = step - EARLY - 1
                    if 0 <= t < TB:
                        (add_residual, form_output)[layer](t, use_at[("P", t)] % 2)
                    if EARLY <= step < HEADS:
                        dve.wait_ge(exp_ready, TB * (layer * HEADS + step + 1))
                        dve.wait_ge(av_done, layer * HEADS + step - 2)
                        dve.tensor_copy(prob_high[:, step % 3], prob[:, step % 2]).then_inc(high_probs, 1)
                        for kt in range(len(pool_low(step)), TB):
                            low_probs(dve, layer, step, kt, low_probs_v)
                    if layer == 0 and step == LN2_STEP:
                        dve.wait_ge(hid_ready, TB)
                        moments(hid, 1e-5, range(0, TB))
                    if layer == 0 and step == LN3_STEP:
                        second_norm(0)
                if layer == 0:
                    normalised(4, xn, y0, y_ready, range(0, TB))

            dve.wait_ge(in_txt, 32)
            moments(hid, 1e-5, range(2, NT, TB))
            dve.memset(x_b[D2:D2 + 1, :], 1.0)
            dve.memset(att_b[D2:D2 + 1, :], 1.0)
            dve.memset(nat_q[:], 0.0)
            dve.memset(nat_k[:], 1.0).then_inc(consts_ready, 1)
            dve.memset(v_sb[:, 0:TB].bitcast(F32), 0.0)
            normalised(0, hid, xn, xn_ready, range(2, NT, TB))
            dve.memset(v_sb[:, TB:NT].bitcast(F32), 0.0).then_inc(v_zeroed, 1)
            dve.wait_ge(v_zeroed, 1)
            for hl in range(GROUP):
                dve.memset(v_sb[:, :, hl:H:GROUP, GW + hl:GW + hl + 1].bitcast(F32), 1.0)
            dve.wait_ge(in_wide, 16)
            dve.wait_ge(in_tok, 112)
            dve.tensor_copy(eye_bf[:], eye)
            dve.tensor_copy(pick_col[:], wide_sb[:, P + 512:P + 512 + 15])
            dve.tensor_copy(masks[:], small_sb[0:E, 512 + E * P:MERGE])
            link(dve.tensor_copy(spread[:], small_sb[0:3 * E, 512:512 + E * P].rearrange("p (e n) -> p e n", e=E)))
            project(0, 0, 2)
            dve.wait_ge(got1, 8 * 16)
            dve.tensor_copy(own1[:], gat1[:].rearrange("p j (b c) -> p b j c", b=B)).then_inc(apart, 1)
            dve.wait_ge(got2, 2 * 16)
            dve.tensor_copy(own2[:], gat2[:].rearrange("p j (b c) -> p b j c", b=B)).then_inc(apart, 1)
            dve.wait_ge(pe_tok, 1)
            dve.tensor_copy(turned1[:], psum[0:96, 0, 0:B * P].rearrange("p (b j g) -> p j b g", b=B, j=2)).then_inc(ev_tok, 1)
            dve.wait_ge(pe_tok, 2)
            dve.tensor_copy(turned2[:], psum[0:96, 1, 0:B * P].rearrange("p (b j g) -> p j b g", b=B, j=8)).then_inc(ev_tok, 1)
            dve.wait_ge(pe_tok, 3)
            dve.tensor_copy(level1[:], psum[:, 2, 0:EMBED]).then_inc(ev_tok, 1)
            dve.wait_ge(pe_tok, 4)
            dve.tensor_copy(level2[:], psum[0:32, 3, 0:EMBED]).then_inc(ev_tok, 1)
            add_halves()
            image_part(0)
            project(0, 2, 4)
            image_part(1)
            project(0, 4, 6)
            attention(0)

            def softmax(b):
                tiles = slice(b * TB, (b + 1) * TB)
                g, total = gate[:, tiles], gsum[:, tiles]
                wide_of = lambda one: one.rearrange("p (t o) -> p t o", o=1).to_broadcast([P, TB, E])
                dve.wait_ge(logits_done, b + 1)
                logits = psum[:, 6 + b, b * TB * E:(b + 1) * TB * E].rearrange("p (t e) -> p t e", e=E)
                link(dve.tensor_reduce(top[:, tiles], logits, AX_X, ALU.max))
                dve.tensor_tensor(g, logits, wide_of(top[:, tiles]), ALU.subtract).then_inc(logits_in, 1)
                dve.wait_ge(exp4_ready, b + 1)
                link(dve.tensor_reduce(total, g, AX_X, ALU.add))
                link(dve.reciprocal(total, total))
                link(dve.tensor_tensor(g, g, wide_of(total), ALU.mult))
                link(dve.tensor_copy(part[:, tiles, 0, :], g))
                link(dve.tensor_tensor(rest[:, tiles, 0, :], g, part[:, tiles, 0, :], ALU.subtract))
                link(dve.tensor_copy(part[:, tiles, 1, :], rest[:, tiles, 0, :]))
                link(dve.tensor_tensor(rest[:, tiles, 1, :], rest[:, tiles, 0, :], part[:, tiles, 1, :], ALU.subtract))
                dve.tensor_copy(part[:, tiles, 2, :], rest[:, tiles, 1, :]).then_inc(parts_ready, 1)

            def compare(b):
                for n in range(E * TB):
                    e, mt = divmod(n, TB)
                    dve.wait_ge(gate_all_ready, b * E + e + 1)
                    if n >= 4:
                        dve.wait_ge(counted, b * E * TB + n - 3)
                    dve.tensor_scalar(beats[:, n % 4, :], gate_all[:, b, e, :], gate[:, TB * b + mt, e:e + 1], None,
                                      ALU.is_lt).then_inc(beats_ready, 1)

            def choose(b):
                dve.memset(ones_row[:], 1.0)
                dve.wait_ge(counted, (b + 1) * E * TB)
                rank = psum[0:E, 6, 0:SEQ]
                link(dve.tensor_scalar(inside[:], rank, float(CAP), None, ALU.is_lt))
                link(dve.tensor_tensor(place[:], rank, inside[:], ALU.mult))
                link(dve.tensor_reduce(last_rank[:], place[:], AX_X, ALU.max))
                dve.tensor_scalar(room[:], last_rank[:], -1.0, float(CAP), ALU.mult, ALU.add)
                link(dve.tensor_scalar(at_edge[:], rank, last_rank[:, 0:1], None, ALU.is_equal))
                link(dve.tensor_tensor_scan(place[:], ones_row[:], at_edge[:], 0.0, ALU.mult, ALU.add))
                link(dve.tensor_tensor(place[:], place[:], at_edge[:], ALU.mult))
                dve.scalar_tensor_tensor(chosen[:], place[:], room[:, 0:1], inside[:], ALU.is_le, ALU.mult)\
                   .then_inc(chosen_ready, 1)

            def expert_input(b, bank):
                tok = slice(b * SEQ, (b + 1) * SEQ)
                dve.wait_ge(turned, turn_at["Y", (b + 1) * TB - 1] + 1)
                dve.wait_ge(coef_psum, b + 1)
                dve.tensor_tensor(x_a[:, tok], x_a[:, tok], psum[:, bank, 0:SEQ], ALU.mult)
                dve.tensor_tensor(x_b[:, tok], x_b[:, tok], psum[0:D2 + 1, bank + 1, 0:SEQ], ALU.mult).then_inc(hin_ready, 1)

            def output_weights(b):
                tiles = slice(b * TB, (b + 1) * TB)
                dve.wait_ge(chosen_psum, b + 1)
                picked = psum[:, 6, 0:TB * E].rearrange("p (q e) -> p q e", e=E)
                link(dve.tensor_tensor(weight[:, tiles], gate[:, tiles], picked, ALU.mult))
                for e in range(E - 2, -1, -1):
                    link(dve.tensor_tensor(weight[:, tiles, e], weight[:, tiles, e], weight[:, tiles, e + 1], ALU.add))
                for e in range(E):
                    n = BLOCKS[e + 1] - BLOCKS[e]
                    last = dve.tensor_copy(weight_d[:, tiles, BLOCKS[e]:BLOCKS[e + 1]],
                                           weight[:, tiles, e:e + 1].to_broadcast([P, TB, n]))
                last.then_inc(weight_ready, 1)

            softmax(0)
            for t in range(TB, NT):
                add_residual(t, t % 2)
            dve.wait_ge(hid_ready, NT)
            moments(hid, 1e-5, range(TB, NT))
            compare(0)
            second_norm(1)
            choose(0)
            normalised(6, xn, y0, y_ready, range(TB, NT))
            expert_input(0, 0)
            softmax(1)
            output_weights(0)
            compare(1)
            choose(1)
            expert_input(1, 6)
            output_weights(1)
            project(1, 0, NT)
            attention(1)

            for t in range(TB, NT):
                form_output(t, t % 2)


def kernel(x, txt, L0_tok_W0, L0_tok_b0, L0_tok_W1, L0_tok_b1, L0_tok_W2, L0_tok_b2, L0_tok_Wf, L0_tok_bf,
           L0_tok_idx0, L0_tok_idx1, L0_tok_idx2, L0_attn_w_qkv, L0_attn_b_qkv, L0_attn_w_out, L0_attn_b_out,
           L0_ffn_w_router, L0_ffn_gamma1, L0_ffn_beta1, L0_ffn_w1, L0_ffn_b1, L0_ffn_w2, L0_ffn_b2):
    import concourse.bacc as bacc
    from concourse.bass_utils import run_bass_kernel_spmd

    a = {k: np.asarray(v) for k, v in locals().items() if k not in ("bacc", "run_bass_kernel_spmd")}
    x = a["x"]

    def patches(p):
        h = IMG // p
        t = x.reshape(B, CH, h, p, h, p).transpose(2, 4, 0, 3, 5, 1)
        return t.reshape(h * h, B * p * p * CH)

    def index(name, shape, order):
        i = a[name].view(np.uint32)
        return i.reshape(shape).transpose(order)

    wide, small = constants()
    bias = lambda w, b: np.concatenate([w, b[None, :]], axis=0)
    arrays = {
        "rows0": patches(1), "rows1": patches(2), "rows2": patches(4),
        "idx0": index("L0_tok_idx0", (2, P, GP), (1, 0, 2)).reshape(P, 32),
        "idx1": index("L0_tok_idx1", (64, 2, 8), (1, 0, 2)).reshape(P, 8),
        "idx2": index("L0_tok_idx2", (16, 8, 2), (1, 0, 2)).reshape(P, 2),
        "w0": a["L0_tok_W0"].T,
        "w1": a["L0_tok_W1"].T.reshape(2, 96, EMBED).transpose(1, 0, 2),
        "w2": a["L0_tok_W2"].T.reshape(8, 96, EMBED).transpose(1, 0, 2),
        "tok_bias": np.stack([a["L0_tok_b0"], a["L0_tok_b1"], a["L0_tok_b2"]], axis=1),
        "wf": a["L0_tok_Wf"].T.reshape(3, EMBED, D).transpose(1, 0, 2),
        "bf": a["L0_tok_bf"][None, :],
        "txt": a["txt"],
        "wqkv": bias(a["L0_attn_w_qkv"], a["L0_attn_b_qkv"]),
        "wout": bias(a["L0_attn_w_out"], a["L0_attn_b_out"]),
        "wr": a["L0_ffn_w_router"].T,
        "gb": np.stack([a["L0_ffn_gamma1"], a["L0_ffn_beta1"]], axis=1),
        "fc1": bias(a["L0_ffn_w1"].T, a["L0_ffn_b1"]),
        "fc2": bias(a["L0_ffn_w2"].T, a["L0_ffn_b2"]),
        "wide": wide, "small": small,
    }
    arrays = {k: np.ascontiguousarray(v) for k, v in arrays.items()}
    nc = bacc.Bacc("TRN2", target_bir_lowering=False, num_devices=1)
    args = [nc.dram_tensor(k, v.shape, mybir.dt.from_np(v.dtype), kind="ExternalInput").ap() for k, v in arrays.items()]
    out = nc.dram_tensor("out", (B, SEQ, D), F32, kind="ExternalOutput").ap()
    early_fusion(nc, *args, out)
    r = run_bass_kernel_spmd(nc, [arrays], core_ids=[0])
    return r.results[0]["out"]
```
